# Optimizing a Trainium2 kernel written in Bass

```python
import numpy as np
import jax
import jax.numpy as jnp

def _softmax(x, axis=-1):
    return jax.nn.softmax(x, axis=axis)

def _gelu(x):
    return jax.nn.gelu(x, approximate=True)

def _silu(x):
    return jax.nn.silu(x)

def _sigmoid(x):
    return jax.nn.sigmoid(x)

def _layernorm(x, axis=-1, eps=1e-05):
    m = jnp.mean(x, axis=axis, keepdims=True)
    v = jnp.var(x, axis=axis, keepdims=True)
    return (x - m) / jnp.sqrt(v + eps)

def _scatter_add(tgt, idx, src, axis=0):
    return tgt.at[idx].add(src)

def _segment_sum(src, seg, n):
    return jax.ops.segment_sum(src, seg, n)
kernel_name = 'mk_macaron_d1_jaxref_r4_70113e'

def setup_inputs(seed: int=0):
    np.random.seed(seed)
    _w = jnp.asarray

    def _L0_attn_setup():
        import jax, jax.numpy as jnp
        import numpy as np
        B, S, D = (2, 512, 256)
        H, DH = (16, 64)
        DQL, DKVL = (128, 128)
        DR = 64
        TOPK = 64
        LN_EPS = 1e-05
        ROPE_BASE = 10000.0

        def _rope_tables(seq_len, dim):
            inv_freq = 1.0 / ROPE_BASE ** (np.arange(0, dim, 2, dtype=np.float32) / dim)
            t = np.arange(seq_len, dtype=np.float32)
            freqs = np.outer(t, inv_freq)
            cos = np.concatenate([np.cos(freqs), np.cos(freqs)], -1)[:, ::2]
            sin = np.concatenate([np.sin(freqs), np.sin(freqs)], -1)[:, ::2]
            return (jnp.asarray(cos), jnp.asarray(sin))

        def _apply_rope_subspace(x, d_rope):
            s = x.shape[-2]
            cos, sin = _rope_tables(s, d_rope)
            xr, xp = (x[..., :d_rope], x[..., d_rope:])
            e, o = (xr[..., 0::2], xr[..., 1::2])
            rot = jnp.stack([e * cos - o * sin, e * sin + o * cos], axis=-1).reshape(xr.shape)
            return jnp.concatenate([rot, xp], axis=-1)

        def _reference_tuple_inner(x, w_down_q, w_down_kv, w_up_q, w_up_k, w_up_v, w_out, ln_scale, ln_bias):
            b, s, d = x.shape
            residual = x
            mu = jnp.mean(x, axis=-1, keepdims=True)
            var = jnp.mean((x - mu) ** 2, axis=-1, keepdims=True)
            h = (x - mu) * jax.lax.rsqrt(var + LN_EPS) * ln_scale + ln_bias
            c_q = h @ w_down_q.T
            c_kv = h @ w_down_kv.T
            q = (c_q @ w_up_q.T).reshape(b, s, H, DH).transpose(0, 2, 1, 3)
            k = (c_kv @ w_up_k.T).reshape(b, s, H, DH).transpose(0, 2, 1, 3)
            v = (c_kv @ w_up_v.T).reshape(b, s, H, DH).transpose(0, 2, 1, 3)
            q = _apply_rope_subspace(q, DR)
            k = _apply_rope_subspace(k, DR)
            scale = 1.0 / np.sqrt(DH).astype(np.float32)
            scores = jnp.einsum('bhqd,bhkd->bhqk', q, k) * scale
            _, indices = jax.lax.top_k(scores, min(TOPK, s))
            attn = jax.nn.softmax(scores, axis=-1)
            out = jnp.einsum('bhqk,bhkd->bhqd', attn, v)
            out = out.transpose(0, 2, 1, 3).reshape(b, s, H * DH)
            out = out @ w_out.T + residual
            return (out, indices.astype(jnp.int64))
        key = jax.random.key(seed)
        ks = jax.random.split(key, 7)
        init = lambda k, shape: jax.random.normal(k, shape, jnp.float32) * 0.02
        return {'x': jax.random.normal(ks[0], (B, S, D), jnp.float32), 'w_down_q': init(ks[1], (DQL, D)), 'w_down_kv': init(ks[2], (DKVL, D)), 'w_up_q': init(ks[3], (H * DH, DQL)), 'w_up_k': init(ks[4], (H * DH, DKVL)), 'w_up_v': init(ks[5], (H * DH, DKVL)), 'w_out': init(ks[6], (D, H * DH)), 'ln_scale': jnp.ones((D,), jnp.float32), 'ln_bias': jnp.zeros((D,), jnp.float32)}
    _L0_attn_in = _L0_attn_setup()

    def _L0_ffn_setup():
        import jax, jax.numpy as jnp
        import numpy as np
        B, S, D, E, H, K = (4, 512, 256, 8, 128, 2)
        key = jax.random.key(seed)
        ks = jax.random.split(key, 11)
        sc = 0.02
        return {'x': jax.random.normal(ks[0], (B, S, D), dtype=jnp.float32), 'gate_W': jax.random.normal(ks[1], (D, E), dtype=jnp.float32) * sc, 'W1': jax.random.normal(ks[2], (E, D, H), dtype=jnp.float32) * sc, 'b1': jnp.zeros((E, H), dtype=jnp.float32), 'W2': jax.random.normal(ks[3], (E, H, D), dtype=jnp.float32) * sc, 'b2': jnp.zeros((E, D), dtype=jnp.float32), 'Ws1': jax.random.normal(ks[4], (D, H), dtype=jnp.float32) * sc, 'bs1': jnp.zeros((H,), dtype=jnp.float32), 'Ws2': jax.random.normal(ks[5], (H, D), dtype=jnp.float32) * sc, 'bs2': jnp.zeros((D,), dtype=jnp.float32), 'route_scale': jnp.ones((), dtype=jnp.float32)}
    _L0_ffn_in = _L0_ffn_setup()
    _d = {'L0_attn_x': _L0_attn_in['x'], 'L0_attn_w_down_q': _L0_attn_in['w_down_q'], 'L0_attn_w_down_kv': _L0_attn_in['w_down_kv'], 'L0_attn_w_up_q': _L0_attn_in['w_up_q'], 'L0_attn_w_up_k': _L0_attn_in['w_up_k'], 'L0_attn_w_up_v': _L0_attn_in['w_up_v'], 'L0_attn_w_out': _L0_attn_in['w_out'], 'L0_attn_ln_scale': _L0_attn_in['ln_scale'], 'L0_attn_ln_bias': _L0_attn_in['ln_bias'], 'L0_ffn_gate_W': _L0_ffn_in['gate_W'], 'L0_ffn_W1': _L0_ffn_in['W1'], 'L0_ffn_b1': _L0_ffn_in['b1'], 'L0_ffn_W2': _L0_ffn_in['W2'], 'L0_ffn_b2': _L0_ffn_in['b2'], 'L0_ffn_Ws1': _L0_ffn_in['Ws1'], 'L0_ffn_bs1': _L0_ffn_in['bs1'], 'L0_ffn_Ws2': _L0_ffn_in['Ws2'], 'L0_ffn_bs2': _L0_ffn_in['bs2'], 'L0_ffn_route_scale': _L0_ffn_in['route_scale']}
    _x0 = _d['L0_attn_x']
    _d['L0_attn_x'] = jax.random.normal(jax.random.fold_in(jax.random.key(seed), 1), (8, 1024, 256), dtype=_x0.dtype)
    del _x0
    return _d

def reference(L0_attn_x, L0_attn_w_down_q, L0_attn_w_down_kv, L0_attn_w_up_q, L0_attn_w_up_k, L0_attn_w_up_v, L0_attn_w_out, L0_attn_ln_scale, L0_attn_ln_bias, L0_ffn_gate_W, L0_ffn_W1, L0_ffn_b1, L0_ffn_W2, L0_ffn_b2, L0_ffn_Ws1, L0_ffn_bs1, L0_ffn_Ws2, L0_ffn_bs2, L0_ffn_route_scale):

    def _L0_attn_ref(x, w_down_q, w_down_kv, w_up_q, w_up_k, w_up_v, w_out, ln_scale, ln_bias):
        import jax, jax.numpy as jnp
        import numpy as np
        B, S, D = (2, 512, 256)
        H, DH = (16, 64)
        DQL, DKVL = (128, 128)
        DR = 64
        TOPK = 64
        LN_EPS = 1e-05
        ROPE_BASE = 10000.0

        def _rope_tables(seq_len, dim):
            inv_freq = 1.0 / ROPE_BASE ** (np.arange(0, dim, 2, dtype=np.float32) / dim)
            t = np.arange(seq_len, dtype=np.float32)
            freqs = np.outer(t, inv_freq)
            cos = np.concatenate([np.cos(freqs), np.cos(freqs)], -1)[:, ::2]
            sin = np.concatenate([np.sin(freqs), np.sin(freqs)], -1)[:, ::2]
            return (jnp.asarray(cos), jnp.asarray(sin))

        def _apply_rope_subspace(x, d_rope):
            s = x.shape[-2]
            cos, sin = _rope_tables(s, d_rope)
            xr, xp = (x[..., :d_rope], x[..., d_rope:])
            e, o = (xr[..., 0::2], xr[..., 1::2])
            rot = jnp.stack([e * cos - o * sin, e * sin + o * cos], axis=-1).reshape(xr.shape)
            return jnp.concatenate([rot, xp], axis=-1)

        def _reference_tuple_inner(x, w_down_q, w_down_kv, w_up_q, w_up_k, w_up_v, w_out, ln_scale, ln_bias):
            b, s, d = x.shape
            residual = x
            mu = jnp.mean(x, axis=-1, keepdims=True)
            var = jnp.mean((x - mu) ** 2, axis=-1, keepdims=True)
            h = (x - mu) * jax.lax.rsqrt(var + LN_EPS) * ln_scale + ln_bias
            c_q = h @ w_down_q.T
            c_kv = h @ w_down_kv.T
            q = (c_q @ w_up_q.T).reshape(b, s, H, DH).transpose(0, 2, 1, 3)
            k = (c_kv @ w_up_k.T).reshape(b, s, H, DH).transpose(0, 2, 1, 3)
            v = (c_kv @ w_up_v.T).reshape(b, s, H, DH).transpose(0, 2, 1, 3)
            q = _apply_rope_subspace(q, DR)
            k = _apply_rope_subspace(k, DR)
            scale = 1.0 / np.sqrt(DH).astype(np.float32)
            scores = jnp.einsum('bhqd,bhkd->bhqk', q, k) * scale
            _, indices = jax.lax.top_k(scores, min(TOPK, s))
            attn = jax.nn.softmax(scores, axis=-1)
            out = jnp.einsum('bhqk,bhkd->bhqd', attn, v)
            out = out.transpose(0, 2, 1, 3).reshape(b, s, H * DH)
            out = out @ w_out.T + residual
            return (out, indices.astype(jnp.int64))
        return _reference_tuple_inner(x, w_down_q, w_down_kv, w_up_q, w_up_k, w_up_v, w_out, ln_scale, ln_bias)[0]

    def _L0_ffn_ref(x, gate_W, W1, b1, W2, b2, Ws1, bs1, Ws2, bs2, route_scale):
        import jax, jax.numpy as jnp
        import numpy as np
        B, S, D, E, H, K = (4, 512, 256, 8, 128, 2)
        scores = jax.nn.sigmoid(x @ gate_W) * route_scale
        topk_scores, topk_idx = jax.lax.top_k(scores, K)
        topk_w = topk_scores / topk_scores.sum(-1, keepdims=True)
        onehot = jax.nn.one_hot(topk_idx, E, dtype=x.dtype)
        gate_full = jnp.einsum('bsk,bske->bse', topk_w, onehot)
        h = jax.nn.gelu(jnp.einsum('bsd,edh->bseh', x, W1) + b1, approximate=False)
        y = jnp.einsum('bseh,ehd->bsed', h, W2) + b2
        expert_out = jnp.einsum('bse,bsed->bsd', gate_full, y)
        shared = jax.nn.gelu(x @ Ws1 + bs1, approximate=False) @ Ws2 + bs2
        return expert_out + shared
    x = L0_attn_x
    x = x + 0.5 * _L0_ffn_ref(_layernorm(x, axis=-1), L0_ffn_gate_W, L0_ffn_W1, L0_ffn_b1, L0_ffn_W2, L0_ffn_b2, L0_ffn_Ws1, L0_ffn_bs1, L0_ffn_Ws2, L0_ffn_bs2, L0_ffn_route_scale)
    x = x + _L0_attn_ref(_layernorm(x, axis=-1), L0_attn_w_down_q, L0_attn_w_down_kv, L0_attn_w_up_q, L0_attn_w_up_k, L0_attn_w_up_v, L0_attn_w_out, L0_attn_ln_scale, L0_attn_ln_bias)
    x = x + 0.5 * _L0_ffn_ref(_layernorm(x, axis=-1), L0_ffn_gate_W, L0_ffn_W1, L0_ffn_b1, L0_ffn_W2, L0_ffn_b2, L0_ffn_Ws1, L0_ffn_bs1, L0_ffn_Ws2, L0_ffn_bs2, L0_ffn_route_scale)
    return x

_drawn_inputs = setup_inputs


def setup_inputs(seed=0):
    import zlib

    import numpy as np

    out = dict(_drawn_inputs(seed))
    spreads = {'L0_attn_ln_scale': (1.0, 0.6),
     'L0_attn_ln_bias': (0.0, 0.8),
     'L0_ffn_b1': (0.0, 0.8),
     'L0_ffn_b2': (0.0, 0.1),
     'L0_ffn_bs1': (0.0, 0.8),
     'L0_ffn_bs2': (0.0, 0.1)}
    factors = {'L0_attn_w_down_q': 8.0,
     'L0_attn_w_down_kv': 8.0,
     'L0_attn_w_up_q': 8.0,
     'L0_attn_w_up_k': 8.0,
     'L0_attn_w_up_v': 8.0,
     'L0_attn_w_out': 8.0,
     'L0_ffn_W1': 2.791}
    for name, (base, spread) in spreads.items():
        noise = np.random.default_rng([zlib.crc32(name.encode()), seed]).standard_normal(out[name].shape)
        drawn = base * np.exp(spread * noise) if base else spread * noise
        out[name] = jnp.asarray(drawn.astype(out[name].dtype))
    for name, factor in factors.items():
        out[name] = (out[name] * factor).astype(out[name].dtype)
    return out
```

```python
import concourse.bass as bass
from concourse import mybir
from contextlib import ExitStack


class Count:

    def __init__(self, handle):
        self.handle, self.value = handle, 0


class Queue:

    def __init__(self):
        self.items, self.seen = [], {}

    def wait(self, *marks):
        for mark in marks:
            if mark is not None and self.seen.get(mark[0], 0) < mark[1]:
                self.items.append((None, mark))
                self.seen[mark[0]] = mark[1]

    def do(self, emit, count=None, by=1):
        if count is None:
            self.items.append((emit, None))
            return None
        count.value += by
        self.items.append((emit, (count, by)))
        return (count, count.value)

    def play(self, eng):
        for emit, mark in self.items:
            if emit is None:
                eng.wait_ge(mark[0].handle, mark[1])
            else:
                ins = emit(eng)
                if mark is not None:
                    ins.then_inc(mark[0].handle, mark[1])


class Ring:

    def __init__(self, banks):
        self.banks, self.free, self.n = banks, [None] * len(banks), 0

    def take(self):
        k = self.n % len(self.banks)
        assert self.free[k] != "held"
        mark, self.free[k] = self.free[k], "held"
        self.n += 1
        return k, self.banks[k], mark

    def give(self, k, mark):
        self.free[k] = mark


def mm(out, lhsT, rhs, start, stop, shared=False):
    if shared:
        return lambda e: e.matmul(out, lhsT, rhs, start=start, stop=stop, skip_group_check=True)
    return lambda e: e.matmul(out, lhsT, rhs, start=start, stop=stop)


def tr(out, in_, ident):
    return lambda e: e.transpose(out, in_, ident)


def macaron_kernel(nc, a, out):
    fp32, fp32r, bf16 = mybir.dt.float32, mybir.dt.float32r, mybir.dt.bfloat16
    ALU, ACT, AX = mybir.AluOpType, mybir.ActivationFunctionType, mybir.AxisListType

    NB, S, D = 8, 1024, 256
    T = S // 128
    E, H = 8, 128
    NE = E + 1
    G = 2 * E + 1
    NP = 8
    GP = 2
    EPS = 1e-5
    SCALE = 0.125
    BIG = 3.0e38

    def tt(o, x, y, op):
        return lambda e: e.tensor_tensor(o, x, y, op)

    def ts(o, x, s1, s2, op0, op1=None):
        if op1 is None:
            return lambda e: e.tensor_scalar(o, x, s1, None, op0)
        return lambda e: e.tensor_scalar(o, x, s1, s2, op0, op1)

    def stt(o, x, s, y, op0, op1):
        return lambda e: e.scalar_tensor_tensor(out=o, in0=x, scalar=s, in1=y, op0=op0, op1=op1)

    def red(o, x, op, negate=False):
        return lambda e: e.tensor_reduce(o, x, AX.X, op, negate=negate)

    def cp(o, x):
        return lambda e: e.tensor_copy(o, x)

    def act(o, x, f, **k):
        return lambda e: e.activation(o, x, f, **k)

    def dma(o, x):
        return lambda e: e.dma_start(o, x)

    def rows(x, b):
        return x[b * S:(b + 1) * S, :].rearrange("(i p) d -> p i d", p=128)

    x1 = nc.dram_tensor("x1", [NB * S, D], fp32, kind="Internal").ap()
    x2 = nc.dram_tensor("x2", [NB * S, D], fp32, kind="Internal").ap()

    ctx = ExitStack()
    PS = [ctx.enter_context(nc.psum_tensor(f"PS{i}", [128, 1024], fp32)) for i in range(2)]
    PO = ctx.enter_context(nc.psum_tensor("PO", [128, 1024], fp32))
    PM = [ctx.enter_context(nc.psum_tensor(f"PM{i}", [128, 512], fp32)) for i in range(2)]

    def norm_steps(q, c, pool, c_rs, ST, MV, RS, HALF, X, Y, loaded, y_free):
        q.wait(loaded)
        for i in range(T):
            st = q.do(lambda e, i=i: e.bn_stats(ST[:, i, :], X[:, i, :]), c)
            if i % 2:
                yield
        q.wait(st)
        for i in range(T):
            mv = q.do(lambda e, i=i: e.bn_aggr(MV[:, i, :], ST[:, i, :]), c)
        pool.wait(mv)
        var = pool.do(ts(RS[:, :], MV[:, :, 1], EPS, None, ALU.add), c_rs)
        pool.wait(var)
        rs = pool.do(tt(RS[:, :], RS[:, :], HALF[:, :], ALU.pow), c_rs)
        q.wait(rs, y_free)
        yield
        for i in range(T):
            y = q.do(ts(Y[:, i, :], X[:, i, :], MV[:, i, 0:1], RS[:, i:i + 1], ALU.subtract, ALU.mult), c)
            if i % 2:
                yield
        return y

    def ffn(tag, src, dst):
        with ExitStack() as local:
            def sb(name, shape, dt):
                return local.enter_context(nc.sbuf_tensor(tag + name, shape, dt))

            def cnt(name):
                return Count(ctx.enter_context(nc.semaphore(tag + name)))

            PE, ACTQ, DVE, POOL, SP = Queue(), Queue(), Queue(), Queue(), Queue()
            W1f, W2 = sb("W1f", [128, NE * 2 * H], fp32), sb("W2", [128, NE * D], fp32)
            W1h, W1l = sb("W1h", [128, NE, 2, H], fp32r), sb("W1l", [128, NE, 2, H], fp32r)
            gWf = sb("gWf", [128, 2 * E], fp32)
            gWh, gWl = sb("gWh", [128, 2, E], fp32r), sb("gWl", [128, 2, E], fp32r)
            b1, b2 = sb("b1", [128, NE], fp32), sb("b2", [G, D], fp32)
            rsc, desc = sb("rsc", [128, 1], fp32), sb("desc", [128, E], fp32)
            ident = sb("ident", [128, 128], fp32)
            self_, selr = sb("self", [2 * E, E * 128], fp32), sb("selr", [2 * E, E, 128], fp32r)
            XB = [sb(f"XB{i}", [128, T, D], fp32) for i in range(2)]
            XN = sb("XN", [128, T, D], fp32)
            XH = [sb(f"XH{i}", [128, 2, S], fp32r) for i in range(2)]
            XL = [sb(f"XL{i}", [128, 2, S], fp32r) for i in range(2)]
            ST, MV, RS = sb("ST", [128, T, 6], fp32), sb("MV", [128, T, 2], fp32), sb("RS", [128, T], fp32)
            HALF = sb("HALF", [128, T], fp32)
            EG, SC = sb("EG", [128, T * E], fp32), sb("SC", [128, T, E], fp32)
            O1, O2 = sb("O1", [128, T, E], fp32), sb("O2", [128, T, E], fp32)
            EQ, S2 = sb("EQ", [128, T, E], fp32), sb("S2", [128, T, E], fp32)
            M1, M2, F1 = sb("M1", [128, T], fp32), sb("M2", [128, T], fp32), sb("F1", [128, T], fp32)
            DN, WA, WB = sb("DN", [128, T], fp32), sb("WA", [128, T], fp32), sb("WB", [128, T], fp32)
            GF = sb("GF", [128, T, E], fp32)
            G2 = sb("G2", [128, T, G], fp32r)
            GT = [sb(f"GT{i}", [G, S], fp32r) for i in range(2)]
            HB = [sb(f"HB{i}", [128, 512], fp32) for i in range(3)]
            GH = [sb(f"GH{i}", [128, 512], fp32) for i in range(3)]

            c_w, c_ld, c_st = cnt("w"), [cnt("ld0"), cnt("ld1")], [cnt("st0"), cnt("st1")]
            c_dve, c_gate, c_rs = cnt("dve"), cnt("gate"), cnt("rs")
            c_wp, c_wa, c_tr, c_xh, c_xl = cnt("wp"), cnt("wa"), cnt("tr"), cnt("xh"), cnt("xl")
            c_lg, c_eg, c_gt, c_gc = cnt("lg"), cnt("eg"), cnt("gt"), cnt("gc")
            c_up, c_gb, c_hb, c_gh, c_dn, c_x = cnt("up"), cnt("gb"), cnt("hb"), cnt("gh"), cnt("dn"), cnt("x")

            hring = Ring([PS[0][:, 0:512], PS[0][:, 512:1024], PS[1][:, 0:512], PS[1][:, 512:1024]])
            ring = Ring([PM[0], PM[1]])
            ld, st = {}, {}

            def load(b):
                SP.wait(st.get(b - 2))
                ld[b] = SP.do(dma(XB[b % 2][:, :, :], rows(src, b)), c_ld[b % 2], 16)

            load(0)
            for t, name in ((ident, "ident"), (W1f, "W1"), (gWf, "gate"), (b1, "b1"), (rsc, "rs"), (desc, "desc"),
                            (self_, "sel"), (W2, "W2"), (b2, "b2")):
                w = SP.do(dma(t[:, :], a[name]), c_w, 16)
            load(1)

            ACTQ.wait(w)
            ACTQ.do(act(gWh[:, :, :], gWf[:, :].rearrange("p (c e) -> p c e", c=2), ACT.Copy), c_wa)
            ACTQ.do(act(selr[:, :, :], self_[:, :].rearrange("p (e n) -> p e n", e=E), ACT.Copy), c_wa)
            wa = ACTQ.do(act(W1h[:, :, :, :], W1f[:, :].rearrange("p (e c n) -> p e c n", e=NE, c=2), ACT.Copy), c_wa)
            POOL.wait(POOL.do(lambda e: e.memset(HALF[:, :], -0.5), c_wp))
            POOL.wait(w, wa)
            POOL.do(tt(gWl[:, :, :], gWf[:, :].rearrange("p (c e) -> p c e", c=2), gWh[:, :, :], ALU.subtract), c_wp)
            ones = POOL.do(lambda e: e.memset(G2[:, :, G - 1:G].bitcast(fp32), 1.0), c_wp)
            wp = POOL.do(tt(W1l[:, :, :, :], W1f[:, :].rearrange("p (e c n) -> p e c n", e=NE, c=2), W1h[:, :, :, :],
                            ALU.subtract), c_wp)

            up_last, tr_last, gc, gt_read, logit_read = {}, {}, {}, {}, {}
            xsplit = {}

            def prep(b):
                y = yield from norm_steps(DVE, c_dve, POOL, c_rs, ST, MV, RS, HALF, XB[b % 2], XN, ld[b], tr_last.get(b - 1))
                for t in range(2):
                    for c in range(2):
                        k, bank, free = hring.take()
                        PE.wait(free, y, w)
                        for i in range(4):
                            t_ = PE.do(tr(bank[:, i * 128:(i + 1) * 128], XN[:, 4 * t + i, c * 128:(c + 1) * 128],
                                          ident[:, :]), c_tr if i == 3 else None)
                        sl = slice(t * 512, (t + 1) * 512)
                        ACTQ.wait(t_, up_last.get(b - 2))
                        xh = ACTQ.do(act(XH[b % 2][:, c, sl], bank[:, :], ACT.Copy), c_xh)
                        DVE.wait(xh, up_last.get(b - 2))
                        xl = DVE.do(tt(XL[b % 2][:, c, sl], bank[:, :], XH[b % 2][:, c, sl], ALU.subtract), c_xl)
                        hring.give(k, xl)
                        tr_last[b] = t_
                        yield
                xsplit[b] = xl
                k, bank, free = ring.take()
                PE.wait(free, xl, wa, wp)
                for i in range(T):
                    for c in range(2):
                        tok = slice(i * 128, (i + 1) * 128)
                        o = bank[:, i * E:(i + 1) * E]
                        PE.do(mm(o, XH[b % 2][:, c, tok], gWh[:, c, :], c == 0, False))
                        PE.do(mm(o, XH[b % 2][:, c, tok], gWl[:, c, :], False, False))
                        lg = PE.do(mm(o, XL[b % 2][:, c, tok], gWh[:, c, :], False, c == 1),
                                   c_lg if i == T - 1 and c == 1 else None)
                ACTQ.wait(lg, logit_read.get(b - 1))
                eg = ACTQ.do(act(EG[:, :], bank[:, 0:T * E], ACT.Exp, scale=-1.0), c_eg)
                ring.give(k, eg)
                yield
                DVE.wait(eg, gt_read.get(b - 1), w)

                def step(f):
                    DVE.wait(DVE.do(f, c_gate))

                def wide(x):
                    return x[:, :].unsqueeze(2).broadcast_to([128, T, E])

                order = desc[:, :].unsqueeze(1).broadcast_to([128, T, E])
                step(ts(EG[:, :], EG[:, :], 1.0, None, ALU.add))
                logit_read[b] = DVE.do(lambda e: e.reciprocal(SC[:, :, :], EG[:, :].rearrange("p (t e) -> p t e", e=E)), c_gate)
                DVE.wait(logit_read[b])
                step(ts(SC[:, :, :], SC[:, :, :], rsc[:, 0:1], None, ALU.mult))
                yield

                def pick(scores, best, hot):
                    step(red(best[:, :], scores[:, :, :], ALU.max))
                    step(tt(EQ[:, :, :], scores[:, :, :], wide(best), ALU.is_equal))
                    step(tt(EQ[:, :, :], EQ[:, :, :], order, ALU.mult))
                    step(red(F1[:, :], EQ[:, :, :], ALU.max))
                    step(tt(hot[:, :, :], EQ[:, :, :], wide(F1), ALU.is_equal))

                pick(SC, M1, O1)
                yield
                step(stt(S2[:, :, :], O1[:, :, :], -BIG, SC[:, :, :], ALU.mult, ALU.add))
                pick(S2, M2, O2)
                yield
                step(tt(DN[:, :], M1[:, :], M2[:, :], ALU.add))
                step(lambda e: e.reciprocal(DN[:, :], DN[:, :]))
                step(tt(WA[:, :], M1[:, :], DN[:, :], ALU.mult))
                step(tt(WB[:, :], M2[:, :], DN[:, :], ALU.mult))
                step(tt(O1[:, :, :], O1[:, :, :], wide(WA), ALU.mult))
                step(tt(O2[:, :, :], O2[:, :, :], wide(WB), ALU.mult))
                step(tt(GF[:, :, :], O1[:, :, :], O2[:, :, :], ALU.add))
                step(cp(G2[:, :, 0:E], GF[:, :, :]))
                g = DVE.do(tt(G2[:, :, E:2 * E], GF[:, :, :], G2[:, :, 0:E], ALU.subtract), c_gate)
                yield
                for t in range(2):
                    k, bank, free = ring.take()
                    PE.wait(free, g, ones)
                    for i in range(4):
                        gt = PE.do(tr(bank[0:G, i * 128:(i + 1) * 128], G2[:, 4 * t + i, :].bitcast(fp32), ident[:, :]),
                                   c_gt if i == 3 else None)
                    ACTQ.wait(gt, dn_last.get(b - 2))
                    gc[b] = ACTQ.do(act(GT[b % 2][:, t * 512:(t + 1) * 512], bank[0:G, :], ACT.Copy), c_gc)
                    ring.give(k, gc[b])
                gt_read[b] = gt
                yield

            dn_last, dn_of, xo = {}, {}, None
            gh_of, hb_of = {}, {}
            n = 0

            def advance(it):
                next(it, None)

            for _ in prep(0):
                pass
            for b in range(NB):
                it = prep(b + 1) if b + 1 < NB else iter(())
                for t in range(2):
                    sl = slice(t * 512, (t + 1) * 512)

                    def down(e, m, b=b, t=t):
                        PE.wait(gh_of[m], xo if e == 0 else None, w)
                        for i in range(4):
                            d = PE.do(mm(PO[:, i * D:(i + 1) * D], GH[m % 3][:, i * 128:(i + 1) * 128],
                                         W2[:, e * D:(e + 1) * D], e == 0 and i % 2 == 0, False, True),
                                      c_dn if i == 3 else None)
                        dn_of[m] = d

                    for e in range(NE):
                        PE.wait(xsplit[b])
                        k, bank, free = hring.take()
                        PE.wait(free, wp)
                        for c in range(2):
                            PE.do(mm(bank[:, :], W1l[:, e, c, :], XH[b % 2][:, c, sl], c == 0, False))
                            PE.do(mm(bank[:, :], W1h[:, e, c, :], XL[b % 2][:, c, sl], False, False))
                            u = PE.do(mm(bank[:, :], W1h[:, e, c, :], XH[b % 2][:, c, sl], False, c == 1),
                                      c_up if c == 1 else None)
                        up_last[b] = u
                        if e < E:
                            ACTQ.wait(u, gh_of.get(n - 3))
                            hb = ACTQ.do(act(HB[n % 3][:, :], bank[:, :], ACT.Gelu, bias=b1[:, e:e + 1]), c_hb)
                            hring.give(k, hb)
                            k, bank, free = ring.take()
                            PE.wait(free, gc[b])
                            gb = PE.do(mm(bank[:, :], selr[:, e, :], GT[b % 2][0:2 * E, sl], True, True), c_gb)
                            DVE.wait(hb, gb, dn_of.get(n - 3))
                            gh_of[n] = DVE.do(tt(GH[n % 3][:, :], HB[n % 3][:, :], bank[:, :], ALU.mult), c_gh)
                            ring.give(k, gh_of[n])
                        else:
                            ACTQ.wait(u, dn_of.get(n - 3))
                            gh_of[n] = ACTQ.do(act(GH[n % 3][:, :], bank[:, :], ACT.Gelu, bias=b1[:, e:e + 1]), c_hb)
                            hring.give(k, gh_of[n])
                        if e >= 1:
                            down(e - 1, n - 1)
                        advance(it)
                        n += 1
                    down(NE - 1, n - 1)
                    for i in range(4):
                        tok = slice(t * 512 + i * 128, t * 512 + (i + 1) * 128)
                        d = PE.do(mm(PO[:, i * D:(i + 1) * D], GT[b % 2][:, tok].bitcast(fp32), b2[:, :], False, True, True),
                                  c_dn if i == 3 else None)
                    dn_last[b] = d
                    DVE.wait(d)
                    xo = DVE.do(stt(XB[b % 2][:, 4 * t:4 * t + 4, :], PO[:, :].rearrange("p (i d) -> p i d", d=D), 0.5,
                                    XB[b % 2][:, 4 * t:4 * t + 4, :], ALU.mult, ALU.add), c_x)
                for _ in it:
                    pass
                SP.wait(xo)
                st[b] = SP.do(dma(rows(dst, b), XB[b % 2][:, :, :]), c_st[b % 2], 16)
                if b + 2 < NB:
                    load(b + 2)
            SP.wait(st[NB - 2], st[NB - 1])
            run(PE, ACTQ, DVE, POOL, SP)

    def run(PE, ACTQ, DVE, POOL, SP):
        with nc.Block() as block:
            @block.tensor
            def _(eng):
                PE.play(eng)

            @block.scalar
            def _(eng):
                ACTQ.play(eng)

            @block.vector
            def _(eng):
                DVE.play(eng)

            @block.gpsimd
            def _(eng):
                POOL.play(eng)

            @block.sync
            def _(eng):
                SP.play(eng)

    def attention(src, dst):
        with ExitStack() as local:
            def sb(name, shape, dt):
                return local.enter_context(nc.sbuf_tensor("at" + name, shape, dt))

            def cnt(name):
                return Count(ctx.enter_context(nc.semaphore("at" + name)))

            PE, ACTQ, DVE, POOL, SP = Queue(), Queue(), Queue(), Queue(), Queue()
            WD = [sb("WDq", [128, 2 * 128], fp32), sb("WDkv", [128, 2 * 128], fp32)]
            WU = [[sb("WQ", [128, S], fp32), sb("WQS", [128, S], fp32)], [sb("WK", [128, S], fp32), sb("WKS", [128, S], fp32)]]
            WV, WO = sb("WV", [128, S], fp32), sb("WO", [128, NP * D], fp32)
            COS, SIN = sb("COS", [128, S], fp32), sb("SIN", [128, S], fp32)
            lns = sb("lns", [128, 4], fp32)
            ident, identb, ones = sb("ident", [128, 128], fp32), sb("identb", [128, 128], bf16), sb("ones", [128, 64], fp32)
            XB = [sb(f"XB{i}", [128, T, D], fp32) for i in range(2)]
            Y = sb("Y", [128, T, D], fp32)
            ST, MV, RS = sb("ST", [128, T, 6], fp32), sb("MV", [128, T, 2], fp32), sb("RS", [128, T], fp32)
            HALF = sb("HALF", [128, T], fp32)
            C = [sb("CQ", [128, S], fp32), sb("CKV", [128, S], fp32)]
            U = sb("U", [128, 2, S], fp32)
            VT = [sb(f"VT{i}", [128, 512], fp32) for i in range(2)]
            QA = [[sb(f"QA{i}{h}", [128, S], fp32r) for h in range(2)] for i in range(2)]
            QB = [[sb(f"QB{i}{h}", [128, S], fp32r) for h in range(2)] for i in range(2)]
            KA = [[sb(f"KA{i}{h}", [128, S], fp32r) for h in range(2)] for i in range(2)]
            KB = [[sb(f"KB{i}{h}", [128, S], fp32r) for h in range(2)] for i in range(2)]
            V = [sb(f"V{i}", [128, T, 128], fp32) for i in range(2)]
            PT = [[sb(f"PT{i}{h}", [128, S], fp32) for h in range(2)] for i in range(3)]
            ACC = [[sb(f"ACC{i}{h}", [128, S], fp32) for h in range(2)] for i in range(2)]
            RSUM = sb("RSUM", [128, 512], fp32)
            AT = sb("AT", [128, GP, S], fp32)
            NM, MF = sb("NM", [128, 16, 2], fp32), sb("MF", [128, 16], fp32)
            MC = sb("MC", [128, 16, 2], bf16)

            c_w, c_ld, c_st = cnt("w"), [cnt("ld0"), cnt("ld1")], [cnt("st0"), cnt("st1")]
            c_ini, c_dve, c_rs, c_res = cnt("ini"), cnt("dve"), cnt("rs"), cnt("res")
            c_tr, c_ht, c_dp, c_c = cnt("tr"), cnt("ht"), cnt("dp"), cnt("c")
            c_up, c_rope, c_rot, c_hi, c_lo = cnt("up"), cnt("rope"), cnt("rot"), cnt("hi"), cnt("lo")
            c_vp, c_v, c_mx, c_nm, c_mr, c_mrow = cnt("vp"), cnt("v"), cnt("mx"), cnt("nm"), cnt("mr"), cnt("mrow")
            c_qk, c_exp, c_pv, c_acc, c_o = cnt("qk"), cnt("exp"), cnt("pv"), cnt("acc"), cnt("o")
            c_sum, c_rec, c_at, c_op, c_x = cnt("sum"), cnt("rec"), cnt("atn"), cnt("op"), cnt("x")

            ring = Ring([PM[0], PM[1]])
            ld, st = {}, {}

            def load(b):
                SP.wait(st.get(b - 2))
                ld[b] = SP.do(dma(XB[b % 2][:, :, :], rows(src, b)), c_ld[b % 2], 16)

            load(0)
            for t, name in ((ident, "ident"), (lns, "ln"), (WD[0], "wdq"), (WD[1], "wdkv"), (WU[0][0], "wq"),
                            (WU[0][1], "wqs"), (WU[1][0], "wk"), (WU[1][1], "wks"), (COS, "cos"), (SIN, "sin"),
                            (WV, "wv"), (WO, "wo")):
                w = SP.do(dma(t[:, :], a[name]), c_w, 16)
            load(1)
            POOL.wait(POOL.do(lambda e: e.memset(HALF[:, :], -0.5), c_ini))
            for i in range(2):
                POOL.do(lambda e, i=i: e.memset(KB[i][0][64:96, :].bitcast(fp32), 1.0), c_ini)
                POOL.do(lambda e, i=i: e.memset(QB[i][1][0:64, :].bitcast(fp32), 0.0), c_ini)
                z = POOL.do(lambda e, i=i: e.memset(KB[i][1][0:64, :].bitcast(fp32), 0.0), c_ini)
                POOL.wait(z)
                POOL.do(lambda e, i=i: e.memset(KB[i][1][0:2, :].bitcast(fp32), 1.0), c_ini)
            POOL.do(lambda e: e.memset(ones[:, :], 1.0), c_ini)
            POOL.wait(w)
            ini = POOL.do(cp(identb[:, :], ident[:, :]), c_ini)

            HI = [slice(0, 64), slice(64, 128)]
            KR = [slice(0, 66), slice(0, 128)]
            MROW = [slice(64, 66), slice(0, 2)]
            y_of, res_of, c_of, up_of, lo_of, hi_of, dp_of = {}, {}, {}, {}, {}, {}, {}
            ready, v_of, qk_of, pv_of, mr_of, sum_of, op_of, at_of, o_of, nm_of = {}, {}, {}, {}, {}, {}, {}, {}, {}, {}
            last_rope, rot_used, tr_of = [None, None], {}, {}

            def norms(b):
                y = yield from norm_steps(DVE, c_dve, POOL, c_rs, ST, MV, RS, HALF, XB[b % 2], Y, ld[b], tr_of.get(b - 1))
                POOL.wait(y)
                res_of[b] = POOL.do(tt(XB[b % 2][:, :, :], XB[b % 2][:, :, :], Y[:, :, :], ALU.add), c_res)
                DVE.wait(y)
                y_of[b] = yield from norm_steps(DVE, c_dve, POOL, c_rs, ST, MV, RS, HALF, Y, Y, None, res_of[b])

            def latents(b):
                n0 = 8 * b - 1
                for t in range(2):
                    sl = slice(t * 512, (t + 1) * 512)
                    for c in range(2):
                        k, bank, free = ring.take()
                        PE.wait(free, y_of[b], w)
                        for i in range(4):
                            tr_of[b] = PE.do(tr(bank[:, i * 128:(i + 1) * 128], Y[:, 4 * t + i, c * 128:(c + 1) * 128],
                                                ident[:, :]), c_tr if i == 3 else None)
                        ACTQ.wait(tr_of[b], w, lo_of.get(n0), hi_of.get(n0))
                        ht = ACTQ.do(act(U[:, c, sl], bank[:, :], ACT.Identity, scale=lns[:, c:c + 1],
                                         bias=lns[:, 2 + c:3 + c]), c_ht)
                        ring.give(k, ht)
                        yield
                for t in range(2):
                    sl = slice(t * 512, (t + 1) * 512)
                    for m in range(2):
                        k, bank, free = ring.take()
                        PE.wait(free, ht)
                        for c in range(2):
                            dp_of[b] = PE.do(mm(bank[:, :], WD[m][:, c * 128:(c + 1) * 128], U[:, c, sl], c == 0, c == 1),
                                             c_dp if c == 1 else None)
                        ACTQ.wait(dp_of[b], up_of.get(n0))
                        c_of[b] = ACTQ.do(act(C[m][:, sl], bank[:, :], ACT.Copy), c_c)
                        ring.give(k, c_of[b])
                        yield

            def project(n):
                b, p = divmod(n, NP)
                s = n % 2
                cols = slice(p * 128, (p + 1) * 128)
                for m in range(2):
                    for t in range(2):
                        sl = slice(t * 512, (t + 1) * 512)
                        for r in range(2):
                            k, bank, free = ring.take()
                            PE.wait(free, c_of[b])
                            up = PE.do(mm(bank[:, :], WU[m][r][:, cols], C[m][:, sl], True, True), c_up)
                            if r == 0:
                                DVE.wait(up, w, dp_of[b], lo_of.get(n - 1), hi_of.get(n - 1))
                                rope = DVE.do(tt(U[:, m, sl], bank[:, :], COS[:, sl], ALU.mult), c_rope)
                            else:
                                DVE.wait(up, last_rope[t])
                                rope = DVE.do(tt(VT[t][:, :], bank[:, :], SIN[:, sl], ALU.mult), c_rope)
                            ring.give(k, rope)
                            if r == 1:
                                POOL.wait(rope)
                                rot = POOL.do(tt(U[:, m, sl], U[:, m, sl], VT[t][:, :], ALU.add), c_rot)
                                last_rope[t] = rot
                            yield
                    ACTQ.wait(rot, qk_of.get(n - 2), ini)
                    if m == 0:
                        hi = [ACTQ.do(act(QA[s][h][o, :], U[HI[h], 0, :], ACT.Copy), c_hi) for h in range(2) for o in HI]
                        DVE.wait(hi[-1], qk_of.get(n - 2), ini)
                        for h in range(2):
                            lo = DVE.do(tt(QB[s][h][HI[h], :], U[HI[h], 0, :], QA[s][h][HI[h], :], ALU.subtract), c_lo)
                    else:
                        hi = [ACTQ.do(act(K[s][h][HI[h], :], U[HI[h], 1, :], ACT.Copy), c_hi) for K in (KA, KB)
                              for h in range(2)]
                        DVE.wait(hi[1], qk_of.get(n - 2))
                        for h in range(2):
                            lo = DVE.do(tt(KA[s][h][HI[1 - h], :], U[HI[h], 1, :], KA[s][h][HI[h], :], ALU.subtract), c_lo)
                    yield
                lo_of[n], hi_of[n], up_of[n] = lo, hi[-1], up

            def values(n):
                b, p = divmod(n, NP)
                cols = slice(p * 128, (p + 1) * 128)
                for t in range(2):
                    k, bank, free = ring.take()
                    PE.wait(free, c_of[b])
                    for i in range(4):
                        vp = PE.do(mm(bank[:, i * 128:(i + 1) * 128], C[1][:, (4 * t + i) * 128:(4 * t + i + 1) * 128],
                                      WV[:, cols], True, True), c_vp if i == 3 else None)
                    ACTQ.wait(vp, pv_of.get(n - 2))
                    v_of[n] = ACTQ.do(act(V[n % 2][:, 4 * t:4 * t + 4, :], bank[:, :].rearrange("p (i d) -> p i d", d=128),
                                          ACT.Copy), c_v)
                    ring.give(k, v_of[n])
                    up_of[n] = vp
                    yield

            def maxima(n):
                s = n % 2
                PE.wait(hi_of[n])
                for q in range(T):
                    for t in range(2):
                        for h in range(2):
                            k, bank, free = ring.take()
                            PE.wait(free)
                            mx = PE.do(mm(bank[:, :], QA[s][h][HI[h], q * 128:(q + 1) * 128],
                                          KA[s][h][HI[h], t * 512:(t + 1) * 512], True, True), c_mx)
                            DVE.wait(mx, nm_of.get(n - 1))
                            nm = DVE.do(red(NM[:, h * T + q, t:t + 1], bank[:, :], ALU.max, True), c_nm)
                            ring.give(k, nm)
                            yield
                DVE.wait(nm, mr_of.get(n - 1))
                f = DVE.do(red(MF[:, :], NM[:, :, :], ALU.min), c_nm)
                DVE.wait(f)
                f = DVE.do(cp(MC[:, :, 0], MF[:, :]), c_nm)
                DVE.wait(f)
                nm_of[n] = DVE.do(tt(MC[:, :, 1], MF[:, :], MC[:, :, 0], ALU.subtract), c_nm)
                yield
                for t in range(2):
                    k, bank, free = ring.take()
                    PE.wait(free, nm_of[n], ini)
                    for q in range(4):
                        for h in range(2):
                            mr_of[n] = PE.do(mm(bank[MROW[h], q * 128:(q + 1) * 128], MC[:, h * T + 4 * t + q, :],
                                                identb[:, :], True, True), c_mr if q == 3 and h == 1 else None)
                    ACTQ.wait(mr_of[n])
                    for h in range(2):
                        row = ACTQ.do(act(QB[s][h][MROW[h], t * 512:(t + 1) * 512], bank[MROW[h], :], ACT.Copy), c_mrow)
                    ring.give(k, row)
                    yield
                ready[n] = (row, lo_of[n], hi_of[n])

            def finish(n):
                b, p = divmod(n, NP)
                for t in range(2):
                    sl = slice(t * 512, (t + 1) * 512)
                    k, bank, free = ring.take()
                    PE.wait(free, acc_of[n], ini)
                    for h in range(2):
                        sum_of[n] = PE.do(mm(bank[HI[h], :], ones[:, :], ACC[n % 2][h][:, sl], True, True),
                                          c_sum if h == 1 else None)
                    DVE.wait(sum_of[n], o_of[n], at_of.get(n, at_of.get(n - 1)))
                    rec = DVE.do(lambda e, bank=bank: e.reciprocal(RSUM[:, :], bank[:, :]), c_rec)
                    ring.give(k, rec)
                    DVE.wait(rec)
                    at_of[n] = DVE.do(tt(AT[:, p % GP, sl], AT[:, p % GP, sl], RSUM[:, :], ALU.mult), c_at)
                    yield
                if p % GP == GP - 1:
                    for u in range(4):
                        k, bank, free = ring.take()
                        PE.wait(free, at_of[n])
                        for i in range(2):
                            for q in range(GP):
                                tok = slice((2 * u + i) * 128, (2 * u + i + 1) * 128)
                                op_of[n] = PE.do(mm(bank[:, i * D:(i + 1) * D], AT[:, q, tok],
                                                    WO[:, (p - GP + 1 + q) * D:(p - GP + 2 + q) * D], q == 0, q == GP - 1),
                                                 c_op if i == 1 and q == GP - 1 else None)
                        x = XB[b % 2][:, 2 * u:2 * u + 2, :]
                        DVE.wait(op_of[n], res_of[b], x_of.get((b, u)))
                        x_of[b, u] = DVE.do(tt(x, x, bank[:, :].rearrange("p (i d) -> p i d", d=D), ALU.add), c_x)
                        ring.give(k, x_of[b, u])
                        yield
                    if p == 7:
                        SP.wait(x_of[b, 3])
                        st[b] = SP.do(dma(rows(dst, b), XB[b % 2][:, :, :]), c_st[b % 2], 16)
                        if b + 2 < NB:
                            load(b + 2)

            acc_of, x_of = {}, {}
            s_free, pt_free, tile = [None, None], [None] * 3, 0

            for g in (norms(0), latents(0), project(0), values(0), maxima(0)):
                for _ in g:
                    pass
            NN = NB * NP
            for n in range(NN):
                b, p = divmod(n, NP)
                s = n % 2
                work = []
                if n + 1 < NN:
                    if p == 7:
                        work.append(latents(b + 1))
                    work.append(project(n + 1))
                    if n:
                        work.append(finish(n - 1))
                    work += [values(n + 1), maxima(n + 1)]
                    if p == 6 and b + 1 < NB:
                        work.append(norms(b + 1))
                elif n:
                    work.append(finish(n - 1))
                units = 12 + 2 + 2 + 35 + (8 if p == 7 else 0) + (4 if p % GP == 0 else 0) + (18 if p == 6 else 0)
                points, done = 32, 0

                def chain(work):
                    for g in work:
                        yield from g
                filler = chain(work)

                def fill(k, n=n):
                    nonlocal done
                    while done * points < units * k:
                        next(filler, None)
                        done += 1

                exps = {}

                def pv(j):
                    o_prev = o_of.get(n - 1)
                    PE.wait(v_of[n], exps[j, 0], exps[j, 1], o_prev)
                    base = n * T + j
                    for t in range(2):
                        sl = slice(t * 512, (t + 1) * 512)
                        for h in range(2):
                            m = PE.do(mm(PO[HI[h], sl], V[s][:, j, HI[h]], PT[base % 3][h][:, sl], j == 0, j == T - 1),
                                      c_pv if t == 1 and h == 1 else None)
                        if t == 0:
                            fill(4 * j + 3)
                    pv_of[n] = m
                    pt_pv[base] = m

                pt_pv = {} if n == 0 else pt_pv
                pt_acc = {} if n == 0 else pt_acc
                for j in range(T):
                    base = n * T + j
                    for h in range(2):
                        z = PS[tile % 2]
                        PE.wait(s_free[tile % 2], *ready[n])
                        for K_, Q_, r in ((KA, QA, slice(0, 128)), (KB, QB, KR[h])):
                            for t in range(2):
                                sl = slice(t * 512, (t + 1) * 512)
                                qk = PE.do(mm(z[:, sl], K_[s][h][r, j * 128:(j + 1) * 128], Q_[s][h][r, sl],
                                              K_ is KA, K_ is KB), c_qk if K_ is KB and t == 1 else None)
                        qk_of[n] = qk
                        ACTQ.wait(qk, pt_pv.get(base - 3), pt_acc.get(base - 3))
                        exps[j, h] = ACTQ.do(act(PT[base % 3][h][:, :], z[:, :], ACT.Exp, scale=SCALE), c_exp)
                        s_free[tile % 2] = exps[j, h]
                        tile += 1
                        fill(4 * j + h + 1)
                    if j >= 1:
                        for h in range(2):
                            POOL.wait(exps[j, h], sum_of.get(n - 2), pt_acc.get(base - 1) if j > 1 else None)
                            first = PT[(base - 1) % 3][h] if j == 1 else ACC[s][h]
                            ac = POOL.do(tt(ACC[s][h][:, :], first[:, :], PT[base % 3][h][:, :], ALU.add), c_acc)
                        pt_acc[base] = ac
                        if j == 1:
                            pt_acc[base - 1] = ac
                        acc_of[n] = ac
                    if j >= 1:
                        pv(j - 1)
                    fill(4 * j + 4)
                for _ in filler:
                    pass
                pv(T - 1)
                ACTQ.wait(pv_of[n], op_of.get(n - 1 - p % GP))
                o_of[n] = ACTQ.do(act(AT[:, p % GP, :], PO[:, :], ACT.Copy), c_o)
            for _ in finish(NN - 1):
                pass
            SP.wait(st[NB - 2], st[NB - 1])
            run(PE, ACTQ, DVE, POOL, SP)

    ffn("f1", a["x"], x1)
    attention(x1, x2)
    ffn("f2", x2, out)


def _tables(np):
    inv = 1.0 / 10000.0 ** (np.arange(0, 64, 2, dtype=np.float32) / 64)
    freqs = np.outer(np.arange(1024, dtype=np.float32), inv)
    cos = np.concatenate([np.cos(freqs), np.cos(freqs)], -1)[:, ::2]
    sin = np.concatenate([np.sin(freqs), np.sin(freqs)], -1)[:, ::2]
    dim = np.arange(128) % 64 // 2
    sign = np.where(np.arange(128) % 2 == 0, -1.0, 1.0).astype(np.float32)
    return cos[:, dim].T.astype(np.float32), (sin[:, dim].T * sign[:, None]).astype(np.float32)


def kernel(**inputs):
    import numpy as np
    import concourse.bacc as _bacc
    from concourse import mybir as _mybir
    from concourse.bass_utils import run_bass_kernel_spmd as _run

    v = {k: np.asarray(x) for k, x in inputs.items()}
    f = {k[7:]: x for k, x in v.items() if k.startswith("L0_ffn_")}
    t = {k[8:]: x for k, x in v.items() if k.startswith("L0_attn_")}
    cos, sin = _tables(np)
    sel = np.zeros((16, 8, 128), np.float32)
    for e in range(8):
        sel[e, e], sel[8 + e, e] = 1.0, 1.0

    def chunks(w):
        return w.reshape(-1, 128, w.shape[1]).transpose(1, 0, 2).reshape(128, -1)

    def turned(w):
        return w.reshape(512, 2, 128)[:, ::-1].reshape(1024, 128)

    w1 = np.concatenate([f["W1"], f["Ws1"][None]])
    w2 = np.concatenate([f["W2"], f["Ws2"][None]])
    ln = np.concatenate([t["ln_scale"].reshape(2, 128), t["ln_bias"].reshape(2, 128)])
    arrays = {
        "x": t["x"].reshape(8192, 256),
        "W1": w1.reshape(9, 2, 128, 128).transpose(2, 0, 1, 3).reshape(128, -1),
        "W2": w2.transpose(1, 0, 2).reshape(128, -1),
        "gate": chunks(f["gate_W"]),
        "b1": np.concatenate([f["b1"], f["bs1"][None]]).T,
        "b2": np.concatenate([f["b2"], f["b2"], f["bs2"][None]]),
        "rs": np.broadcast_to(f["route_scale"].reshape(1, 1), (128, 1)),
        "desc": np.broadcast_to(np.arange(8, 0, -1, dtype=np.float32), (128, 8)),
        "sel": sel.reshape(16, -1),
        "ident": np.eye(128, dtype=np.float32),
        "ln": ln.T,
        "wdq": chunks(t["w_down_q"].T),
        "wdkv": chunks(t["w_down_kv"].T),
        "wq": t["w_up_q"].T,
        "wqs": turned(t["w_up_q"]).T,
        "wk": t["w_up_k"].T,
        "wks": turned(t["w_up_k"]).T,
        "wv": t["w_up_v"].T,
        "wo": chunks(t["w_out"].T),
        "cos": cos,
        "sin": sin,
    }
    nc = _bacc.Bacc("TRN2", target_bir_lowering=False, num_devices=1)
    args, maps = {}, {}
    for name, x in arrays.items():
        x = np.ascontiguousarray(x)
        maps["in_" + name] = x
        args[name] = nc.dram_tensor("in_" + name, x.shape, _mybir.dt.from_np(x.dtype), kind="ExternalInput").ap()
    out = nc.dram_tensor("out_0", (8192, 256), _mybir.dt.float32, kind="ExternalOutput").ap()
    macaron_kernel(nc, args, out)
    r = _run(nc, [maps], core_ids=[0])
    return r.results[0]["out_0"].reshape(8, 1024, 256)
```

```python
import concourse.bass as bass
from concourse import mybir
from contextlib import ExitStack


class Count:

    def __init__(self, handle):
        self.handle, self.value = handle, 0


class Queue:

    def __init__(self):
        self.items, self.seen = [], {}

    def wait(self, *marks):
        for mark in marks:
            if mark is not None and self.seen.get(mark[0], 0) < mark[1]:
                self.items.append((None, mark))
                self.seen[mark[0]] = mark[1]

    def do(self, emit, count=None, by=1):
        if count is None:
            self.items.append((emit, None))
            return None
        count.value += by
        self.items.append((emit, (count, by)))
        return (count, count.value)

    def play(self, eng):
        for emit, mark in self.items:
            if emit is None:
                eng.wait_ge(mark[0].handle, mark[1])
            else:
                ins = emit(eng)
                if mark is not None:
                    ins.then_inc(mark[0].handle, mark[1])


class Ring:

    def __init__(self, banks):
        self.banks, self.free, self.n = banks, [None] * len(banks), 0

    def take(self):
        k = self.n % len(self.banks)
        assert self.free[k] != "held"
        mark, self.free[k] = self.free[k], "held"
        self.n += 1
        return k, self.banks[k], mark

    def give(self, k, mark):
        self.free[k] = mark


def mm(out, lhsT, rhs, start, stop, shared=False):
    if shared:
        return lambda e: e.matmul(out, lhsT, rhs, start=start, stop=stop, skip_group_check=True)
    return lambda e: e.matmul(out, lhsT, rhs, start=start, stop=stop)


def tr(out, in_, ident):
    return lambda e: e.transpose(out, in_, ident)


def macaron_kernel(nc, a, out):
    fp32, fp32r, bf16 = mybir.dt.float32, mybir.dt.float32r, mybir.dt.bfloat16
    ALU, ACT, AX = mybir.AluOpType, mybir.ActivationFunctionType, mybir.AxisListType

    NB, S, D = 8, 1024, 256
    T = S // 128
    E, H = 8, 128
    NE = E + 1
    G = 2 * E + 1
    NP = 8
    GP = 2
    NH = 4
    NX = 3
    LAG = 3
    EPS = 1e-5
    SCALE = 0.125
    BIG = 3.0e38

    def tt(o, x, y, op):
        return lambda e: e.tensor_tensor(o, x, y, op)

    def ts(o, x, s1, s2, op0, op1=None):
        if op1 is None:
            return lambda e: e.tensor_scalar(o, x, s1, None, op0)
        return lambda e: e.tensor_scalar(o, x, s1, s2, op0, op1)

    def stt(o, x, s, y, op0, op1):
        return lambda e: e.scalar_tensor_tensor(out=o, in0=x, scalar=s, in1=y, op0=op0, op1=op1)

    def red(o, x, op, negate=False):
        return lambda e: e.tensor_reduce(o, x, AX.X, op, negate=negate)

    def cp(o, x):
        return lambda e: e.tensor_copy(o, x)

    def act(o, x, f, **k):
        return lambda e: e.activation(o, x, f, **k)

    def dma(o, x):
        return lambda e: e.dma_start(o, x)

    def rows(x, b):
        return x[b * S:(b + 1) * S, :].rearrange("(i p) d -> p i d", p=128)

    x1 = nc.dram_tensor("x1", [NB * S, D], fp32, kind="Internal").ap()
    x2 = nc.dram_tensor("x2", [NB * S, D], fp32, kind="Internal").ap()

    ctx = ExitStack()
    PO = ctx.enter_context(nc.psum_tensor("PO", [128, 1024], fp32))
    PS = [ctx.enter_context(nc.psum_tensor(f"PS{i}", [128, 512], fp32)) for i in range(2)]
    PM = [ctx.enter_context(nc.psum_tensor(f"PM{i}", [128, 512], fp32)) for i in range(4)]

    def norm_steps(q, c, pool, c_rs, ST, MV, RS, HALF, X, Y, loaded, y_free):
        q.wait(loaded)
        for i in range(T):
            st = q.do(lambda e, i=i: e.bn_stats(ST[:, i, :], X[:, i, :]), c)
            if i % 2:
                yield
        q.wait(st)
        for i in range(T):
            mv = q.do(lambda e, i=i: e.bn_aggr(MV[:, i, :], ST[:, i, :]), c)
        pool.wait(mv)
        var = pool.do(ts(RS[:, :], MV[:, :, 1], EPS, None, ALU.add), c_rs)
        pool.wait(var)
        rs = pool.do(tt(RS[:, :], RS[:, :], HALF[:, :], ALU.pow), c_rs)
        for _ in range(3):
            yield
        q.wait(rs, y_free)
        for i in range(T):
            y = q.do(ts(Y[:, i, :], X[:, i, :], MV[:, i, 0:1], RS[:, i:i + 1], ALU.subtract, ALU.mult), c)
            if i % 2:
                yield
        return y

    def ffn(tag, src, dst):
        with ExitStack() as local:
            def sb(name, shape, dt):
                return local.enter_context(nc.sbuf_tensor(tag + name, shape, dt))

            def cnt(name):
                return Count(ctx.enter_context(nc.semaphore(tag + name)))

            PE, ACTQ, DVE, POOL, SP = Queue(), Queue(), Queue(), Queue(), Queue()
            W1f, W2f = sb("W1f", [128, NE * 2 * H], fp32), sb("W2f", [128, NE * D], fp32)
            W2h, W2l = sb("W2h", [128, NE * D], fp32r), sb("W2l", [128, NE * D], fp32r)
            W1h, W1l = sb("W1h", [128, NE, 2, H], fp32r), sb("W1l", [128, NE, 2, H], fp32r)
            gWf = sb("gWf", [128, 2 * E], fp32)
            gWp, LT = sb("gWp", [128, 2, 128], fp32r), sb("LT", [2 * E, S], fp32)
            b1, b2f = sb("b1", [128, NE], fp32), sb("b2f", [G, D], fp32)
            b2h, b2l = sb("b2h", [G, D], fp32r), sb("b2l", [G, D], fp32r)
            rsc, desc = sb("rsc", [128, 1], fp32), sb("desc", [128, E], fp32)
            ident = sb("ident", [128, 128], fp32)
            self_, selr = sb("self", [2 * E, E * 128], fp32), sb("selr", [2 * E, E, 128], fp32r)
            XB = [sb(f"XB{i}", [128, T, D], fp32) for i in range(NX)]
            XN = sb("XN", [128, T, D], fp32)
            XH = [sb(f"XH{i}", [128, 2, S], fp32r) for i in range(2)]
            XL = [sb(f"XL{i}", [128, 2, S], fp32r) for i in range(2)]
            ST, MV, RS = sb("ST", [128, T, 6], fp32), sb("MV", [128, T, 2], fp32), sb("RS", [128, T], fp32)
            HALF = sb("HALF", [128, T], fp32)
            EG, SC = sb("EG", [128, T * E], fp32), sb("SC", [128, T, E], fp32)
            O1, O2 = sb("O1", [128, T, E], fp32), sb("O2", [128, T, E], fp32)
            EQ, S2 = sb("EQ", [128, T, E], fp32), sb("S2", [128, T, E], fp32)
            M1, M2, F1 = sb("M1", [128, T], fp32), sb("M2", [128, T], fp32), sb("F1", [128, T], fp32)
            DN, WA, WB = sb("DN", [128, T], fp32), sb("WA", [128, T], fp32), sb("WB", [128, T], fp32)
            GF = sb("GF", [128, T, E], fp32)
            G2 = sb("G2", [128, T, G], fp32r)
            GT = [sb(f"GT{i}", [G, S], fp32r) for i in range(2)]
            HB = [sb(f"HB{i}", [128, 512], fp32) for i in range(NH)]
            GF32 = [sb(f"GF32{i}", [128, 512], fp32) for i in range(NH)]
            GH = [sb(f"GH{i}", [128, 512], fp32r) for i in range(NH)]
            GL = [sb(f"GL{i}", [128, 512], fp32r) for i in range(NH)]

            c_w, c_ld, c_st = cnt("w"), [cnt(f"ld{i}") for i in range(NX)], [cnt(f"st{i}") for i in range(NX)]
            c_dve, c_gate, c_rs = cnt("dve"), cnt("gate"), cnt("rs")
            c_wp, c_wa, c_tr, c_xh, c_xl = cnt("wp"), cnt("wa"), cnt("tr"), cnt("xh"), cnt("xl")
            c_lt, c_lc, c_lg, c_eg, c_gt, c_gc = cnt("lt"), cnt("lc"), cnt("lg"), cnt("eg"), cnt("gt"), cnt("gc")
            c_up, c_gb, c_hb, c_gf, c_gh, c_gl = cnt("up"), cnt("gb"), cnt("hb"), cnt("gf"), cnt("gh"), cnt("gl")
            c_dn, c_x = cnt("dn"), cnt("x")

            hring = Ring(PS + PM[3:])
            ring = Ring(PM[:3])
            ld, st = {}, {}

            def load(b):
                SP.wait(st.get(b - NX))
                ld[b] = SP.do(dma(XB[b % NX][:, :, :], rows(src, b)), c_ld[b % NX], 16)

            load(0)
            for t, name in ((ident, "ident"), (W1f, "W1"), (gWf, "gate"), (b1, "b1"), (rsc, "rs"), (desc, "desc"),
                            (self_, "sel"), (W2f, "W2"), (b2f, "b2")):
                w = SP.do(dma(t[:, :], a[name]), c_w, 16)
            for b in range(1, NX):
                load(b)

            ACTQ.wait(w)
            z = POOL.do(lambda e: e.memset(gWp[:, :, :].bitcast(fp32), 0.0), c_wp)
            ACTQ.wait(z)
            ACTQ.do(act(gWp[:, :, 0:E], gWf[:, :].rearrange("p (c e) -> p c e", c=2), ACT.Copy), c_wa)
            ACTQ.do(act(selr[:, :, :], self_[:, :].rearrange("p (e n) -> p e n", e=E), ACT.Copy), c_wa)
            wa = ACTQ.do(act(W1h[:, :, :, :], W1f[:, :].rearrange("p (e c n) -> p e c n", e=NE, c=2), ACT.Copy), c_wa)
            POOL.wait(POOL.do(lambda e: e.memset(HALF[:, :], -0.5), c_wp))
            ACTQ.do(act(W2h[:, :], W2f[:, :], ACT.Copy), c_wa)
            wa2 = ACTQ.do(act(b2h[:, :], b2f[:, :], ACT.Copy), c_wa)
            POOL.wait(w, wa)
            POOL.do(tt(gWp[:, :, E:2 * E], gWf[:, :].rearrange("p (c e) -> p c e", c=2), gWp[:, :, 0:E], ALU.subtract), c_wp)
            ones = POOL.do(lambda e: e.memset(G2[:, :, G - 1:G].bitcast(fp32), 1.0), c_wp)
            wp = POOL.do(tt(W1l[:, :, :, :], W1f[:, :].rearrange("p (e c n) -> p e c n", e=NE, c=2), W1h[:, :, :, :],
                            ALU.subtract), c_wp)
            POOL.wait(wa2)
            POOL.do(tt(W2l[:, :], W2f[:, :], W2h[:, :], ALU.subtract), c_wp)
            wp2 = POOL.do(tt(b2l[:, :], b2f[:, :], b2h[:, :], ALU.subtract), c_wp)

            up_last, tr_last, gc, gt_read, logit_read, lg_of = {}, {}, {}, {}, {}, {}
            xsplit = {}

            def prep(b):
                y = yield from norm_steps(DVE, c_dve, POOL, c_rs, ST, MV, RS, HALF, XB[b % NX], XN, ld[b], tr_last.get(b - 1))
                for t in range(2):
                    for c in range(2):
                        k, bank, free = hring.take()
                        PE.wait(free, y, w)
                        for i in range(4):
                            t_ = PE.do(tr(bank[:, i * 128:(i + 1) * 128], XN[:, 4 * t + i, c * 128:(c + 1) * 128],
                                          ident[:, :]), c_tr if i == 3 else None)
                        sl = slice(t * 512, (t + 1) * 512)
                        ACTQ.wait(t_, up_last.get(b - 2))
                        xh = ACTQ.do(act(XH[b % 2][:, c, sl], bank[:, :], ACT.Copy), c_xh)
                        DVE.wait(xh, up_last.get(b - 2))
                        xl = DVE.do(tt(XL[b % 2][:, c, sl], bank[:, :], XH[b % 2][:, c, sl], ALU.subtract), c_xl)
                        hring.give(k, xl)
                        tr_last[b] = t_
                        yield
                xsplit[b] = xl
                yield
                for t in range(2):
                    sl = slice(t * 512, (t + 1) * 512)
                    k, bank, free = ring.take()
                    PE.wait(free, xl, wa, wp)
                    for c in range(2):
                        PE.do(mm(bank[:, :], gWp[:, c, :], XH[b % 2][:, c, sl], c == 0, False))
                        lt = PE.do(mm(bank[:, :], gWp[:, c, :], XL[b % 2][:, c, sl], False, c == 1), c_lt if c == 1 else None)
                    ACTQ.wait(lt, lg_of.get(b - 1))
                    lc = ACTQ.do(act(LT[:, sl], bank[0:2 * E, :], ACT.Copy), c_lc)
                    ring.give(k, lc)
                    yield
                k, bank, free = ring.take()
                PE.wait(free, lc, w)
                for i in range(T):
                    lg_of[b] = PE.do(mm(bank[:, i * E:(i + 1) * E], LT[:, i * 128:(i + 1) * 128],
                                        self_[:, 0:E * 128:128], True, True), c_lg)
                ACTQ.wait(lg_of[b], logit_read.get(b - 1))
                eg = ACTQ.do(act(EG[:, :], bank[:, 0:T * E], ACT.Exp, scale=-1.0), c_eg)
                ring.give(k, eg)
                yield
                DVE.wait(eg, gt_read.get(b - 1), w)

                def step(f):
                    DVE.wait(DVE.do(f, c_gate))

                def wide(x):
                    return x[:, :].unsqueeze(2).broadcast_to([128, T, E])

                order = desc[:, :].unsqueeze(1).broadcast_to([128, T, E])
                step(ts(EG[:, :], EG[:, :], 1.0, None, ALU.add))
                logit_read[b] = DVE.do(lambda e: e.reciprocal(SC[:, :, :], EG[:, :].rearrange("p (t e) -> p t e", e=E)), c_gate)
                DVE.wait(logit_read[b])
                step(ts(SC[:, :, :], SC[:, :, :], rsc[:, 0:1], None, ALU.mult))
                yield

                def pick(scores, best, hot):
                    step(red(best[:, :], scores[:, :, :], ALU.max))
                    step(tt(EQ[:, :, :], scores[:, :, :], wide(best), ALU.is_equal))
                    yield
                    step(tt(EQ[:, :, :], EQ[:, :, :], order, ALU.mult))
                    step(red(F1[:, :], EQ[:, :, :], ALU.max))
                    step(tt(hot[:, :, :], EQ[:, :, :], wide(F1), ALU.is_equal))

                yield from pick(SC, M1, O1)
                yield
                step(stt(S2[:, :, :], O1[:, :, :], -BIG, SC[:, :, :], ALU.mult, ALU.add))
                yield from pick(S2, M2, O2)
                yield
                step(tt(DN[:, :], M1[:, :], M2[:, :], ALU.add))
                step(lambda e: e.reciprocal(DN[:, :], DN[:, :]))
                step(tt(WA[:, :], M1[:, :], DN[:, :], ALU.mult))
                step(tt(WB[:, :], M2[:, :], DN[:, :], ALU.mult))
                yield
                step(tt(O1[:, :, :], O1[:, :, :], wide(WA), ALU.mult))
                step(tt(O2[:, :, :], O2[:, :, :], wide(WB), ALU.mult))
                step(tt(GF[:, :, :], O1[:, :, :], O2[:, :, :], ALU.add))
                yield
                step(cp(G2[:, :, 0:E], GF[:, :, :]))
                g = DVE.do(tt(G2[:, :, E:2 * E], GF[:, :, :], G2[:, :, 0:E], ALU.subtract), c_gate)
                for _ in range(5):
                    yield
                for t in range(2):
                    k, bank, free = ring.take()
                    PE.wait(free, g, ones)
                    for i in range(4):
                        gt = PE.do(tr(bank[0:G, i * 128:(i + 1) * 128], G2[:, 4 * t + i, :].bitcast(fp32), ident[:, :]),
                                   c_gt if i == 3 else None)
                    ACTQ.wait(gt, dn_last.get(b - 2))
                    gc[b] = ACTQ.do(act(GT[b % 2][:, t * 512:(t + 1) * 512], bank[0:G, :], ACT.Copy), c_gc)
                    ring.give(k, gc[b])
                gt_read[b] = gt
                yield

            dn_last, dn_of, xo = {}, {}, None
            gf_of, gl_of = {}, {}
            n = 0

            def split(m):
                if m in gl_of:
                    return
                f32, hi, lo = GF32[m % NH], GH[m % NH], GL[m % NH]
                ACTQ.wait(gf_of[m], dn_of.get(m - NH))
                gh = ACTQ.do(act(hi[:, :], f32[:, :], ACT.Copy), c_gh)
                POOL.wait(gh, dn_of.get(m - NH))
                gl_of[m] = POOL.do(tt(lo[:, :], f32[:, :], hi[:, :], ALU.subtract), c_gl)

            def advance(it):
                next(it, None)

            for _ in prep(0):
                pass
            for b in range(NB):
                it = prep(b + 1) if b + 1 < NB else iter(())
                for t in range(2):
                    sl = slice(t * 512, (t + 1) * 512)

                    def down(e, m):
                        PE.wait(gl_of[m], xo if e == 0 else None, wp2)
                        w2 = slice(e * D, (e + 1) * D)
                        for i in range(4):
                            o, tok = PO[:, i * D:(i + 1) * D], slice(i * 128, (i + 1) * 128)
                            PE.do(mm(o, GH[m % NH][:, tok], W2h[:, w2], e == 0 and i % 2 == 0, False, True))
                            PE.do(mm(o, GH[m % NH][:, tok], W2l[:, w2], False, False, True))
                            dn_of[m] = PE.do(mm(o, GL[m % NH][:, tok], W2h[:, w2], False, False, True), c_dn)

                    for e in range(NE):
                        PE.wait(xsplit[b])
                        k, bank, free = hring.take()
                        PE.wait(free, wp)
                        for c in range(2):
                            PE.do(mm(bank[:, :], W1l[:, e, c, :], XH[b % 2][:, c, sl], c == 0, False))
                            PE.do(mm(bank[:, :], W1h[:, e, c, :], XL[b % 2][:, c, sl], False, False))
                            u = PE.do(mm(bank[:, :], W1h[:, e, c, :], XH[b % 2][:, c, sl], False, c == 1),
                                      c_up if c == 1 else None)
                        up_last[b] = u
                        f32 = GF32[n % NH]
                        if e < E:
                            ACTQ.wait(u, gf_of.get(n - NH))
                            hb = ACTQ.do(act(HB[n % NH][:, :], bank[:, :], ACT.Gelu, bias=b1[:, e:e + 1]), c_hb)
                            hring.give(k, hb)
                            k, bank, free = ring.take()
                            PE.wait(free, gc[b])
                            gb = PE.do(mm(bank[:, :], selr[:, e, :], GT[b % 2][0:2 * E, sl], True, True), c_gb)
                            DVE.wait(hb, gb, gl_of.get(n - NH))
                            gf_of[n] = DVE.do(tt(f32[:, :], HB[n % NH][:, :], bank[:, :], ALU.mult), c_gf)
                            ring.give(k, gf_of[n])
                        else:
                            ACTQ.wait(u, gl_of.get(n - NH))
                            gf_of[n] = ACTQ.do(act(f32[:, :], bank[:, :], ACT.Gelu, bias=b1[:, e:e + 1]), c_hb)
                            hring.give(k, gf_of[n])
                        advance(it)
                        if n:
                            split(n - 1)
                        if e >= LAG:
                            down(e - LAG, n - LAG)
                        advance(it)
                        n += 1
                    split(n - 1)
                    for e in range(NE - LAG, NE):
                        down(e, n - NE + e)
                    for i in range(4):
                        tok = slice(t * 512 + i * 128, t * 512 + (i + 1) * 128)
                        for B in (b2h, b2l):
                            d = PE.do(mm(PO[:, i * D:(i + 1) * D], GT[b % 2][:, tok], B[:, :], False, B is b2l, True),
                                      c_dn)
                    dn_last[b] = d
                    DVE.wait(d)
                    xo = DVE.do(stt(XB[b % NX][:, 4 * t:4 * t + 4, :], PO[:, :].rearrange("p (i d) -> p i d", d=D), 0.5,
                                    XB[b % NX][:, 4 * t:4 * t + 4, :], ALU.mult, ALU.add), c_x)
                for _ in it:
                    pass
                SP.wait(xo)
                st[b] = SP.do(dma(rows(dst, b), XB[b % NX][:, :, :]), c_st[b % NX], 16)
                if b + NX < NB:
                    load(b + NX)
            SP.wait(*(st[b] for b in range(NB - NX, NB)))
            run(PE, ACTQ, DVE, POOL, SP)

    def run(PE, ACTQ, DVE, POOL, SP):
        with nc.Block() as block:
            @block.tensor
            def _(eng):
                PE.play(eng)

            @block.scalar
            def _(eng):
                ACTQ.play(eng)

            @block.vector
            def _(eng):
                DVE.play(eng)

            @block.gpsimd
            def _(eng):
                POOL.play(eng)

            @block.sync
            def _(eng):
                SP.play(eng)

    def attention(src, dst):
        with ExitStack() as local:
            def sb(name, shape, dt):
                return local.enter_context(nc.sbuf_tensor("at" + name, shape, dt))

            def cnt(name):
                return Count(ctx.enter_context(nc.semaphore("at" + name)))

            PE, ACTQ, DVE, POOL, SP = Queue(), Queue(), Queue(), Queue(), Queue()
            WD = [sb("WDq", [128, 2 * 128], fp32), sb("WDkv", [128, 2 * 128], fp32)]
            WU = [[sb("WQ", [128, S], fp32), sb("WQS", [128, S], fp32)], [sb("WK", [128, S], fp32), sb("WKS", [128, S], fp32)]]
            WV, WO = sb("WV", [128, S], fp32), sb("WO", [128, NP * D], fp32)
            COS, SIN = sb("COS", [128, S], fp32), sb("SIN", [128, S], fp32)
            lns = sb("lns", [128, 4], fp32)
            ident, identb, ones = sb("ident", [128, 128], fp32), sb("identb", [128, 128], bf16), sb("ones", [128, 64], fp32)
            XB = [sb(f"XB{i}", [128, T, D], fp32) for i in range(2)]
            Y = sb("Y", [128, T, D], fp32)
            ST, MV, RS = sb("ST", [128, T, 6], fp32), sb("MV", [128, T, 2], fp32), sb("RS", [128, T], fp32)
            HALF = sb("HALF", [128, T], fp32)
            C = [sb("CQ", [128, S], fp32), sb("CKV", [128, S], fp32)]
            U = sb("U", [128, 2, S], fp32)
            VT = [sb(f"VT{i}", [128, 512], fp32) for i in range(2)]
            QA = [[sb(f"QA{i}{h}", [128, S], fp32r) for h in range(2)] for i in range(2)]
            QB = [[sb(f"QB{i}{h}", [128, S], fp32r) for h in range(2)] for i in range(2)]
            KA = [[sb(f"KA{i}{h}", [128, S], fp32r) for h in range(2)] for i in range(2)]
            KB = [[sb(f"KB{i}{h}", [128, S], fp32r) for h in range(2)] for i in range(2)]
            V = [sb(f"V{i}", [128, T, 128], fp32) for i in range(2)]
            PT = [[sb(f"PT{i}{h}", [128, S], fp32) for h in range(2)] for i in range(3)]
            ACC = [[sb(f"ACC{i}{h}", [128, S], fp32) for h in range(2)] for i in range(2)]
            RSUM = sb("RSUM", [128, S], fp32)
            AT = sb("AT", [128, GP, S], fp32)
            NM, MF = sb("NM", [128, 16, 2], fp32), sb("MF", [128, 16], fp32)
            MC = sb("MC", [128, 16, 2], bf16)

            c_w, c_ld, c_st = cnt("w"), [cnt("ld0"), cnt("ld1")], [cnt("st0"), cnt("st1")]
            c_ini, c_dve, c_rs, c_res = cnt("ini"), cnt("dve"), cnt("rs"), cnt("res")
            c_tr, c_ht, c_dp, c_c = cnt("tr"), cnt("ht"), cnt("dp"), cnt("c")
            c_up, c_rope, c_rot, c_hi, c_lo = cnt("up"), cnt("rope"), cnt("rot"), cnt("hi"), cnt("lo")
            c_vp, c_v, c_mx, c_nm, c_mr, c_mrow = cnt("vp"), cnt("v"), cnt("mx"), cnt("nm"), cnt("mr"), cnt("mrow")
            c_qk, c_exp, c_pv, c_acc, c_o = cnt("qk"), cnt("exp"), cnt("pv"), cnt("acc"), cnt("o")
            c_sum, c_rs2, c_rec, c_at, c_op, c_x = cnt("sum"), cnt("rs2"), cnt("rec"), cnt("atn"), cnt("op"), cnt("x")

            ring = Ring(PM)
            ld, st = {}, {}

            def load(b):
                SP.wait(st.get(b - 2))
                ld[b] = SP.do(dma(XB[b % 2][:, :, :], rows(src, b)), c_ld[b % 2], 16)

            load(0)
            for t, name in ((ident, "ident"), (lns, "ln"), (WD[0], "wdq"), (WD[1], "wdkv"), (WU[0][0], "wq"),
                            (WU[0][1], "wqs"), (WU[1][0], "wk"), (WU[1][1], "wks"), (COS, "cos"), (SIN, "sin"),
                            (WV, "wv"), (WO, "wo")):
                w = SP.do(dma(t[:, :], a[name]), c_w, 16)
            load(1)
            POOL.wait(POOL.do(lambda e: e.memset(HALF[:, :], -0.5), c_ini))
            for i in range(2):
                POOL.do(lambda e, i=i: e.memset(KB[i][0][64:96, :].bitcast(fp32), 1.0), c_ini)
                POOL.do(lambda e, i=i: e.memset(QB[i][1][0:64, :].bitcast(fp32), 0.0), c_ini)
                z = POOL.do(lambda e, i=i: e.memset(KB[i][1][0:64, :].bitcast(fp32), 0.0), c_ini)
                POOL.wait(z)
                POOL.do(lambda e, i=i: e.memset(KB[i][1][0:2, :].bitcast(fp32), 1.0), c_ini)
            POOL.do(lambda e: e.memset(ones[:, :], 1.0), c_ini)
            POOL.wait(w)
            ini = POOL.do(cp(identb[:, :], ident[:, :]), c_ini)

            HI = [slice(0, 64), slice(64, 128)]
            KR = [slice(0, 66), slice(0, 128)]
            MROW = [slice(64, 66), slice(0, 2)]
            y_of, res_of, c_of, up_of, lo_of, hi_of, dp_of = {}, {}, {}, {}, {}, {}, {}
            ready, v_of, qk_of, pv_of, mr_of, sum_of, op_of, at_of, o_of, nm_of = {}, {}, {}, {}, {}, {}, {}, {}, {}, {}
            last_rope, rot_of, tr_of = [None, None], {}, {}

            def norms(b):
                y = yield from norm_steps(DVE, c_dve, POOL, c_rs, ST, MV, RS, HALF, XB[b % 2], Y, ld[b], tr_of.get(b - 1))
                POOL.wait(y)
                res_of[b] = POOL.do(tt(XB[b % 2][:, :, :], XB[b % 2][:, :, :], Y[:, :, :], ALU.add), c_res)
                DVE.wait(y)
                y_of[b] = yield from norm_steps(DVE, c_dve, POOL, c_rs, ST, MV, RS, HALF, Y, Y, None, res_of[b])

            def latents(b):
                n0 = 8 * b - 1
                for t in range(2):
                    sl = slice(t * 512, (t + 1) * 512)
                    for c in range(2):
                        k, bank, free = ring.take()
                        PE.wait(free, y_of[b], w)
                        for i in range(4):
                            tr_of[b] = PE.do(tr(bank[:, i * 128:(i + 1) * 128], Y[:, 4 * t + i, c * 128:(c + 1) * 128],
                                                ident[:, :]), c_tr if i == 3 else None)
                        ACTQ.wait(tr_of[b], w, lo_of.get(n0), hi_of.get(n0))
                        ht = ACTQ.do(act(U[:, c, sl], bank[:, :], ACT.Identity, scale=lns[:, c:c + 1],
                                         bias=lns[:, 2 + c:3 + c]), c_ht)
                        ring.give(k, ht)
                        yield
                for t in range(2):
                    sl = slice(t * 512, (t + 1) * 512)
                    for m in range(2):
                        k, bank, free = ring.take()
                        PE.wait(free, ht)
                        for c in range(2):
                            dp_of[b] = PE.do(mm(bank[:, :], WD[m][:, c * 128:(c + 1) * 128], U[:, c, sl], c == 0, c == 1),
                                             c_dp if c == 1 else None)
                        ACTQ.wait(dp_of[b], up_of.get(n0))
                        c_of[b] = ACTQ.do(act(C[m][:, sl], bank[:, :], ACT.Copy), c_c)
                        ring.give(k, c_of[b])
                        yield

            def rotate(n):
                b, p = divmod(n, NP)
                cols = slice(p * 128, (p + 1) * 128)
                for m in range(2):
                    for t in range(2):
                        sl = slice(t * 512, (t + 1) * 512)
                        for r in range(2):
                            k, bank, free = ring.take()
                            PE.wait(free, c_of[b])
                            up = PE.do(mm(bank[:, :], WU[m][r][:, cols], C[m][:, sl], True, True), c_up)
                            if r == 0:
                                DVE.wait(up, w, dp_of[b], lo_of.get(n - 1), hi_of.get(n - 1))
                                rope = DVE.do(tt(U[:, m, sl], bank[:, :], COS[:, sl], ALU.mult), c_rope)
                            else:
                                DVE.wait(up, last_rope[t])
                                rope = DVE.do(tt(VT[t][:, :], bank[:, :], SIN[:, sl], ALU.mult), c_rope)
                            ring.give(k, rope)
                            if r == 1:
                                POOL.wait(rope)
                                rot_of[n, m] = POOL.do(tt(U[:, m, sl], U[:, m, sl], VT[t][:, :], ALU.add), c_rot)
                                last_rope[t] = rot_of[n, m]
                            yield
                up_of[n] = up

            def highs(n):
                s = n % 2
                for m, A in ((0, QA), (1, KA)):
                    for h in range(2):
                        ACTQ.wait(rot_of[n, m], qk_of.get(n - 2))
                        hi_of[n, m, h] = ACTQ.do(act(A[s][h][HI[h], :], U[HI[h], m, :], ACT.Copy), c_hi)
                        yield

            def parts(n):
                s = n % 2
                ACTQ.wait(ini)
                DVE.wait(qk_of.get(n - 2), ini)
                for h in range(2):
                    ACTQ.do(act(QA[s][h][HI[1 - h], :], U[HI[h], 0, :], ACT.Copy), c_hi)
                    yield
                    DVE.wait(hi_of[n, 0, h])
                    DVE.do(tt(QB[s][h][HI[h], :], U[HI[h], 0, :], QA[s][h][HI[h], :], ALU.subtract), c_lo)
                    yield
                    hi_of[n] = ACTQ.do(act(KB[s][h][HI[h], :], U[HI[h], 1, :], ACT.Copy), c_hi)
                    yield
                    DVE.wait(hi_of[n, 1, h])
                    lo_of[n] = DVE.do(tt(KA[s][h][HI[1 - h], :], U[HI[h], 1, :], KA[s][h][HI[h], :], ALU.subtract), c_lo)
                    yield

            def values(n):
                b, p = divmod(n, NP)
                cols = slice(p * 128, (p + 1) * 128)
                for t in range(2):
                    k, bank, free = ring.take()
                    PE.wait(free, c_of[b])
                    for i in range(4):
                        vp = PE.do(mm(bank[:, i * 128:(i + 1) * 128], C[1][:, (4 * t + i) * 128:(4 * t + i + 1) * 128],
                                      WV[:, cols], True, True), c_vp if i == 3 else None)
                    ACTQ.wait(vp, pv_of.get(n - 2))
                    v_of[n] = ACTQ.do(act(V[n % 2][:, 4 * t:4 * t + 4, :], bank[:, :].rearrange("p (i d) -> p i d", d=128),
                                          ACT.Copy), c_v)
                    ring.give(k, v_of[n])
                    up_of[n] = vp
                    yield

            def maxima(n):
                s = n % 2
                PE.wait(hi_of[n, 1, 1])
                for q in range(T):
                    for t in range(2):
                        for h in range(2):
                            k, bank, free = ring.take()
                            PE.wait(free)
                            mx = PE.do(mm(bank[:, :], QA[s][h][HI[h], q * 128:(q + 1) * 128],
                                          KA[s][h][HI[h], t * 512:(t + 1) * 512], True, True), c_mx)
                            DVE.wait(mx, nm_of.get(n - 1))
                            nm = DVE.do(red(NM[:, h * T + q, t:t + 1], bank[:, :], ALU.max, True), c_nm)
                            ring.give(k, nm)
                            yield
                DVE.wait(nm, mr_of.get(n - 1))
                f = DVE.do(red(MF[:, :], NM[:, :, :], ALU.min), c_nm)
                DVE.wait(f)
                f = DVE.do(cp(MC[:, :, 0], MF[:, :]), c_nm)
                DVE.wait(f)
                nm_of[n] = DVE.do(tt(MC[:, :, 1], MF[:, :], MC[:, :, 0], ALU.subtract), c_nm)
                yield
                for t in range(2):
                    k, bank, free = ring.take()
                    PE.wait(free, nm_of[n], ini)
                    for q in range(4):
                        for h in range(2):
                            mr_of[n] = PE.do(mm(bank[MROW[h], q * 128:(q + 1) * 128], MC[:, h * T + 4 * t + q, :],
                                                identb[:, :], True, True), c_mr if q == 3 and h == 1 else None)
                    ACTQ.wait(mr_of[n])
                    for h in range(2):
                        row = ACTQ.do(act(QB[s][h][MROW[h], t * 512:(t + 1) * 512], bank[MROW[h], :], ACT.Copy), c_mrow)
                    ring.give(k, row)
                    yield
                ready[n] = (row, lo_of[n], hi_of[n])

            def sums(n):
                for t in range(2):
                    sl = slice(t * 512, (t + 1) * 512)
                    k, bank, free = ring.take()
                    PE.wait(free, acc_of[n], ini)
                    for h in range(2):
                        sum_of[n] = PE.do(mm(bank[HI[h], :], ones[:, :], ACC[n % 2][h][:, sl], True, True),
                                          c_sum if h == 1 else None)
                    ACTQ.wait(sum_of[n], at_of.get(n - 1))
                    rs_of[n, t] = ACTQ.do(act(RSUM[:, sl], bank[:, :], ACT.Copy), c_rs2)
                    ring.give(k, rs_of[n, t])
                    yield

            def divide(n):
                for u in range(4):
                    sl = slice(u * 256, (u + 1) * 256)
                    DVE.wait(rs_of[n, u // 2])
                    rec = DVE.do(lambda e, sl=sl: e.reciprocal(RSUM[:, sl], RSUM[:, sl]), c_rec)
                    yield
                DVE.wait(rec, o_of[n])
                o = AT[:, n % GP, :]
                at_of[n] = DVE.do(tt(o, o, RSUM[:, :], ALU.mult), c_at)
                yield

            def outward(n):
                b, p = divmod(n, NP)
                for u in range(4):
                    k, bank, free = ring.take()
                    PE.wait(free, at_of[n])
                    for i in range(2):
                        for q in range(GP):
                            tok = slice((2 * u + i) * 128, (2 * u + i + 1) * 128)
                            op_of[n] = PE.do(mm(bank[:, i * D:(i + 1) * D], AT[:, q, tok],
                                                WO[:, (p - GP + 1 + q) * D:(p - GP + 2 + q) * D], q == 0, q == GP - 1),
                                             c_op if i == 1 and q == GP - 1 else None)
                    x = XB[b % 2][:, 2 * u:2 * u + 2, :]
                    DVE.wait(op_of[n], res_of[b], x_of.get((b, u)))
                    x_of[b, u] = DVE.do(tt(x, x, bank[:, :].rearrange("p (i d) -> p i d", d=D), ALU.add), c_x)
                    ring.give(k, x_of[b, u])
                    yield
                if p == NP - 1:
                    SP.wait(x_of[b, 3])
                    st[b] = SP.do(dma(rows(dst, b), XB[b % 2][:, :, :]), c_st[b % 2], 16)
                    if b + 2 < NB:
                        load(b + 2)

            acc_of, x_of, rs_of = {}, {}, {}
            sring = Ring(PS)
            pt_pv, pt_acc = {}, {}

            for g in (norms(0), latents(0), rotate(0), highs(0), parts(0), values(0), maxima(0)):
                for _ in g:
                    pass
            NN = NB * NP
            for n in range(NN):
                b, p = divmod(n, NP)
                s = n % 2
                plan = []
                d = 4 if p == NP - 1 else 0
                if n + 1 < NN:
                    if d:
                        plan.append([latents(b + 1), 8, 0, d, 0])
                    plan += [[rotate(n + 1), 8, d, d + 7, 0], [highs(n + 1), 4, d + 5, d + 9, 0],
                             [parts(n + 1), 8, d + 12, d + 24, 0], [values(n + 1), 2, d + 8, d + 9, 0]]
                if n:
                    plan += [[sums(n - 1), 2, d + 4, d + 5, 0], [divide(n - 1), 5, d + 5, d + 9, 0]]
                if n + 1 < NN:
                    plan.append([maxima(n + 1), 35, d + 10, 30, 0])
                if n and p % GP == 0:
                    plan.append([outward(n - 1), 4, 10, 16, 0])
                if p == NP - 2 and b + 1 < NB:
                    plan.append([norms(b + 1), 22, 8, 31, 0])

                def fill(k):
                    for x in plan:
                        g, total, first, last, done = x
                        if k >= first:
                            due = total if k >= last else total * (k - first + 1) // (last - first + 1)
                            for _ in range(due - done):
                                next(g, None)
                            x[4] = max(due, done)

                exps = {}

                def pv(j):
                    base = n * T + j
                    PE.wait(v_of[n], o_of.get(n - 1))
                    for t in range(2):
                        sl = slice(t * 512, (t + 1) * 512)
                        PE.wait(exps[j, 0, t], exps[j, 1, t])
                        for h in range(2):
                            m = PE.do(mm(PO[HI[h], sl], V[s][:, j, HI[h]], PT[base % 3][h][:, sl], j == 0, j == T - 1),
                                      c_pv if t == 1 and h == 1 else None)
                        if t == 0:
                            fill(4 * j + 2)
                    pv_of[n] = m
                    pt_pv[base] = m

                for j in range(T):
                    base = n * T + j
                    for h in range(2):
                        for t in range(2):
                            sl = slice(t * 512, (t + 1) * 512)
                            k, bank, free = sring.take()
                            PE.wait(free, *ready[n])
                            PE.do(mm(bank[:, :], KA[s][h][:, j * 128:(j + 1) * 128], QA[s][h][:, sl], True, False))
                            qk_of[n] = PE.do(mm(bank[:, :], KB[s][h][KR[h], j * 128:(j + 1) * 128], QB[s][h][KR[h], sl],
                                                False, True), c_qk)
                            ACTQ.wait(qk_of[n], pt_pv.get(base - 3), pt_acc.get(base - 3))
                            exps[j, h, t] = ACTQ.do(act(PT[base % 3][h][:, sl], bank[:, :], ACT.Exp, scale=SCALE), c_exp)
                            sring.give(k, exps[j, h, t])
                        fill(4 * j + h)
                    if j >= 1:
                        for h in range(2):
                            POOL.wait(exps[j, h, 1], sum_of.get(n - 2), pt_acc.get(base - 1) if j > 1 else None)
                            first = PT[(base - 1) % 3][h] if j == 1 else ACC[s][h]
                            pt_acc[base] = POOL.do(tt(ACC[s][h][:, :], first[:, :], PT[base % 3][h][:, :], ALU.add), c_acc)
                        if j == 1:
                            pt_acc[base - 1] = pt_acc[base]
                        acc_of[n] = pt_acc[base]
                        pv(j - 1)
                    fill(4 * j + 3)
                for x in plan:
                    for _ in x[0]:
                        pass
                pv(T - 1)
                ACTQ.wait(pv_of[n], op_of.get(n - 1 - p % GP))
                o_of[n] = ACTQ.do(act(AT[:, p % GP, :], PO[:, :], ACT.Copy), c_o)
            for g in (sums(NN - 1), divide(NN - 1), outward(NN - 1)):
                for _ in g:
                    pass
            SP.wait(st[NB - 2], st[NB - 1])
            run(PE, ACTQ, DVE, POOL, SP)

    ffn("f1", a["x"], x1)
    attention(x1, x2)
    ffn("f2", x2, out)


def _tables(np):
    inv = 1.0 / 10000.0 ** (np.arange(0, 64, 2, dtype=np.float32) / 64)
    freqs = np.outer(np.arange(1024, dtype=np.float32), inv)
    cos = np.concatenate([np.cos(freqs), np.cos(freqs)], -1)[:, ::2]
    sin = np.concatenate([np.sin(freqs), np.sin(freqs)], -1)[:, ::2]
    dim = np.arange(128) % 64 // 2
    sign = np.where(np.arange(128) % 2 == 0, -1.0, 1.0).astype(np.float32)
    return cos[:, dim].T.astype(np.float32), (sin[:, dim].T * sign[:, None]).astype(np.float32)


def kernel(**inputs):
    import numpy as np
    import concourse.bacc as _bacc
    from concourse import mybir as _mybir
    from concourse.bass_utils import run_bass_kernel_spmd as _run

    v = {k: np.asarray(x) for k, x in inputs.items()}
    f = {k[7:]: x for k, x in v.items() if k.startswith("L0_ffn_")}
    t = {k[8:]: x for k, x in v.items() if k.startswith("L0_attn_")}
    cos, sin = _tables(np)
    sel = np.zeros((16, 8, 128), np.float32)
    for e in range(8):
        sel[e, e], sel[8 + e, e] = 1.0, 1.0

    def chunks(w):
        return w.reshape(-1, 128, w.shape[1]).transpose(1, 0, 2).reshape(128, -1)

    def turned(w):
        return w.reshape(512, 2, 128)[:, ::-1].reshape(1024, 128)

    w1 = np.concatenate([f["W1"], f["Ws1"][None]])
    w2 = np.concatenate([f["W2"], f["Ws2"][None]])
    ln = np.concatenate([t["ln_scale"].reshape(2, 128), t["ln_bias"].reshape(2, 128)])
    arrays = {
        "x": t["x"].reshape(8192, 256),
        "W1": w1.reshape(9, 2, 128, 128).transpose(2, 0, 1, 3).reshape(128, -1),
        "W2": w2.transpose(1, 0, 2).reshape(128, -1),
        "gate": chunks(f["gate_W"]),
        "b1": np.concatenate([f["b1"], f["bs1"][None]]).T,
        "b2": np.concatenate([f["b2"], f["b2"], f["bs2"][None]]),
        "rs": np.broadcast_to(f["route_scale"].reshape(1, 1), (128, 1)),
        "desc": np.broadcast_to(np.arange(8, 0, -1, dtype=np.float32), (128, 8)),
        "sel": sel.reshape(16, -1),
        "ident": np.eye(128, dtype=np.float32),
        "ln": ln.T,
        "wdq": chunks(t["w_down_q"].T),
        "wdkv": chunks(t["w_down_kv"].T),
        "wq": t["w_up_q"].T,
        "wqs": turned(t["w_up_q"]).T,
        "wk": t["w_up_k"].T,
        "wks": turned(t["w_up_k"]).T,
        "wv": t["w_up_v"].T,
        "wo": chunks(t["w_out"].T),
        "cos": cos,
        "sin": sin,
    }
    nc = _bacc.Bacc("TRN2", target_bir_lowering=False, num_devices=1)
    args, maps = {}, {}
    for name, x in arrays.items():
        x = np.ascontiguousarray(x)
        maps["in_" + name] = x
        args[name] = nc.dram_tensor("in_" + name, x.shape, _mybir.dt.from_np(x.dtype), kind="ExternalInput").ap()
    out = nc.dram_tensor("out_0", (8192, 256), _mybir.dt.float32, kind="ExternalOutput").ap()
    macaron_kernel(nc, args, out)
    r = _run(nc, [maps], core_ids=[0])
    return r.results[0]["out_0"].reshape(8, 1024, 256)
```

```python
import concourse.bass as bass
from concourse import mybir
from contextlib import ExitStack


class Count:

    def __init__(self, handle):
        self.handle, self.value = handle, 0


class Queue:

    def __init__(self):
        self.items, self.seen, self.last = [], {}, None

    def wait(self, *marks):
        for mark in marks:
            if mark is not None and self.seen.get(mark[0], 0) < mark[1]:
                self.items.append((None, mark))
                self.seen[mark[0]] = mark[1]

    def do(self, emit, count=None, by=1):
        if count is None:
            self.items.append((emit, None))
            return None
        count.value += by
        self.items.append((emit, (count, by)))
        self.last = (count, count.value)
        return self.last

    def play(self, eng):
        for emit, mark in self.items:
            if emit is None:
                eng.wait_ge(mark[0].handle, mark[1])
            else:
                ins = emit(eng)
                if mark is not None:
                    ins.then_inc(mark[0].handle, mark[1])


class Ring:

    def __init__(self, banks):
        self.banks, self.free, self.n = banks, [None] * len(banks), 0

    def take(self):
        k = self.n % len(self.banks)
        assert self.free[k] != "held"
        mark, self.free[k] = self.free[k], "held"
        self.n += 1
        return k, self.banks[k], mark

    def give(self, k, mark):
        self.free[k] = mark


def mm(out, lhsT, rhs, start, stop, shared=False):
    if shared:
        return lambda e: e.matmul(out, lhsT, rhs, start=start, stop=stop, skip_group_check=True)
    return lambda e: e.matmul(out, lhsT, rhs, start=start, stop=stop)


def tr(out, in_, ident):
    return lambda e: e.transpose(out, in_, ident)


def macaron_kernel(nc, a, out):
    fp32, fp32r, bf16 = mybir.dt.float32, mybir.dt.float32r, mybir.dt.bfloat16
    ALU, ACT, AX = mybir.AluOpType, mybir.ActivationFunctionType, mybir.AxisListType

    NB, S, D = 8, 1024, 256
    T = S // 128
    E, H = 8, 128
    NE = E + 1
    G = 2 * E + 1
    GK = 32 + G
    GF0 = 64
    NP = 8
    GP = 2
    NH = 4
    NX = 3
    EPS = 1e-5
    SCALE = 0.125
    BIG = 3.0e38
    P = dict(norms=(-33, -8), latents=(-4, -3), rotate=(-5, 3), highs=(4, 6), parts=(9, 25),
             values=(7, 8), sums=(69, 70), divide=(70, 76), maxima=(11, 29), outward=(78, 83))
    DD = 1
    Y1 = 1
    Y2 = 1
    Y3 = 5
    LAG = 3
    AHEAD = 3

    def tt(o, x, y, op):
        return lambda e: e.tensor_tensor(o, x, y, op)

    def ts(o, x, s1, s2, op0, op1=None):
        if op1 is None:
            return lambda e: e.tensor_scalar(o, x, s1, None, op0)
        return lambda e: e.tensor_scalar(o, x, s1, s2, op0, op1)

    def stt(o, x, s, y, op0, op1):
        return lambda e: e.scalar_tensor_tensor(out=o, in0=x, scalar=s, in1=y, op0=op0, op1=op1)

    def red(o, x, op, negate=False):
        return lambda e: e.tensor_reduce(o, x, AX.X, op, negate=negate)

    def cp(o, x):
        return lambda e: e.tensor_copy(o, x)

    def act(o, x, f, **k):
        return lambda e: e.activation(o, x, f, **k)

    def dma(o, x):
        return lambda e: e.dma_start(o, x)

    def rows(x, b):
        return x[b * S:(b + 1) * S, :].rearrange("(i p) d -> p i d", p=128)

    x1 = nc.dram_tensor("x1", [NB * S, D], fp32, kind="Internal").ap()
    x2 = nc.dram_tensor("x2", [NB * S, D], fp32, kind="Internal").ap()

    ctx = ExitStack()
    PO = ctx.enter_context(nc.psum_tensor("PO", [128, 1024], fp32))
    PS = [ctx.enter_context(nc.psum_tensor(f"PS{i}", [128, 512], fp32)) for i in range(2)]
    PM = [ctx.enter_context(nc.psum_tensor(f"PM{i}", [128, 512], fp32)) for i in range(4)]

    def norm_steps(q, c, pool, c_rs, ST, MV, RS, HALF, X, Y, loaded, y_free, between=None):
        q.wait(loaded)
        for i in range(T):
            st = q.do(lambda e, i=i: e.bn_stats(ST[:, i, :], X[:, i, :]), c)
            if i % 2:
                yield
        q.wait(st)
        for i in range(T):
            mv = q.do(lambda e, i=i: e.bn_aggr(MV[:, i, :], ST[:, i, :]), c)
        pool.wait(mv)
        var = pool.do(ts(RS[:, :], MV[:, :, 1], EPS, None, ALU.add), c_rs)
        pool.wait(var)
        rs = pool.do(tt(RS[:, :], RS[:, :], HALF[:, :], ALU.pow), c_rs)
        if between is not None:
            y_free = between()
        for _ in range(3):
            yield
        q.wait(rs, y_free)
        for i in range(T):
            y = q.do(ts(Y[:, i, :], X[:, i, :], MV[:, i, 0:1], RS[:, i:i + 1], ALU.subtract, ALU.mult), c)
            if i % 2:
                yield
        return y

    def ffn(tag, src, dst):
        with ExitStack() as local:
            def sb(name, shape, dt):
                return local.enter_context(nc.sbuf_tensor(tag + name, shape, dt))

            def cnt(name):
                return Count(ctx.enter_context(nc.semaphore(tag + name)))

            PE, ACTQ, DVE, POOL, SP = Queue(), Queue(), Queue(), Queue(), Queue()
            W2h, W2l = sb("W2h", [128, NE * D], fp32r), sb("W2l", [128, NE * D], fp32r)
            W1h, W1l = sb("W1h", [128, NE, 2, H], fp32r), sb("W1l", [128, NE, 2, H], fp32r)
            gWf = sb("gWf", [128, 2 * E], fp32)
            gWp, LT = sb("gWp", [128, 2, 128], fp32r), sb("LT", [2 * E, S], fp32)
            GB = [sb(f"GB{i}", [128, E, 512], fp32) for i in range(2)]
            W1f, W2f = (g[:, :, :].rearrange("p e n -> p (e n)")[:, 0:NE * 2 * H] for g in GB)
            b1, b2f, b2s = sb("b1", [128, NE], fp32), sb("b2f", [GK, D], fp32), sb("b2s", [GK, D], fp32r)
            rsc, desc = sb("rsc", [128, 1], fp32), sb("desc", [128, E], fp32)
            ident = sb("ident", [128, 128], fp32)
            sel = sb("sel", [2 * E, E], fp32)
            XB = [sb(f"XB{i}", [128, T, D], fp32) for i in range(NX)]
            XN = sb("XN", [128, T, D], fp32)
            XH = [sb(f"XH{i}", [128, 2, S], fp32r) for i in range(2)]
            XL = [sb(f"XL{i}", [128, 2, S], fp32r) for i in range(2)]
            ST, MV, RS = sb("ST", [128, T, 6], fp32), sb("MV", [128, T, 2], fp32), sb("RS", [128, T], fp32)
            HALF = sb("HALF", [128, T], fp32)
            EG, SC = sb("EG", [128, T * E], fp32), sb("SC", [128, T, E], fp32)
            O1, O2 = sb("O1", [128, T, E], fp32), sb("O2", [128, T, E], fp32)
            EQ, S2 = sb("EQ", [128, T, E], fp32), sb("S2", [128, T, E], fp32)
            M1, M2, F1 = sb("M1", [128, T], fp32), sb("M2", [128, T], fp32), sb("F1", [128, T], fp32)
            DN, WA, WB = sb("DN", [128, T], fp32), sb("WA", [128, T], fp32), sb("WB", [128, T], fp32)
            GF = sb("GF", [128, T, E], fp32)
            G2 = sb("G2", [128, T, GF0 + E], fp32r)
            GT = [sb(f"GT{i}", [GK, S], fp32r) for i in range(2)]
            GR = [sb(f"GR{i}", [GF0 + E, S], fp32) for i in range(2)]
            HB = [sb(f"HB{i}", [128, 512], fp32) for i in range(NH)]
            GF32 = [sb(f"GF32{i}", [128, 512], fp32) for i in range(NH)]
            GH = [sb(f"GH{i}", [128, 512], fp32r) for i in range(NH)]
            GL = [sb(f"GL{i}", [128, 512], fp32r) for i in range(NH)]

            c_w, c_ld, c_st = [cnt(f"w{i}") for i in range(3)], [cnt(f"ld{i}") for i in range(NX)], [cnt(f"st{i}") for i in range(NX)]
            c_dve, c_gate, c_rs = cnt("dve"), cnt("gate"), cnt("rs")
            c_wp, c_wa, c_wd, c_tr, c_xh, c_xl = cnt("wp"), cnt("wa"), cnt("wd"), cnt("tr"), cnt("xh"), cnt("xl")
            c_lt, c_lc, c_lg, c_eg, c_gt, c_gc = cnt("lt"), cnt("lc"), cnt("lg"), cnt("eg"), cnt("gt"), cnt("gc")
            c_up, c_gb, c_hb, c_gf, c_gh, c_gl = cnt("up"), [[cnt(f"gb{t}{e}") for e in range(E)] for t in range(2)], cnt("hb"), cnt("gf"), cnt("gh"), cnt("gl")
            c_dn, c_x = cnt("dn"), cnt("x")

            hring = Ring(PS + PM[3:])
            ring = Ring(PM[:3])
            ld, st = {}, {}

            def load(b):
                SP.wait(st.get(b - NX))
                ld[b] = SP.do(dma(XB[b % NX][:, :, :], rows(src, b)), c_ld[b % NX], 16)

            def weights(count, *tensors):
                for t, name in tensors:
                    mark = SP.do(dma(t if t is W1f or t is W2f else t[:, :], a[name]), count, 16)
                return mark

            load(0)
            w = weights(c_w[0], (ident, "ident"), (gWf, "gate"), (sel, "sel"), (rsc, "rs"), (desc, "desc"), (b1, "b1"))
            w1 = weights(c_w[1], (W1f, "W1"))
            w2 = weights(c_w[2], (W2f, "W2"), (b2f, "b2"))
            for b in range(1, NX):
                load(b)

            POOL.wait(POOL.do(lambda e: e.memset(HALF[:, :], -0.5), c_wp))
            z = POOL.do(lambda e: e.memset(gWp[:, :, :].bitcast(fp32), 0.0), c_wp)
            POOL.wait(POOL.do(lambda e: e.memset(G2[:, :, :].bitcast(fp32), 0.0), c_wp))
            for i in (G - 1, GK - 1):
                ones = POOL.do(lambda e, i=i: e.memset(G2[:, :, i:i + 1].bitcast(fp32), 1.0), c_wp)
            ACTQ.wait(w, z)
            gh = ACTQ.do(act(gWp[:, :, 0:E], gWf[:, :].rearrange("p (c e) -> p c e", c=2), ACT.Copy), c_wa)
            ACTQ.wait(w1)
            wa = ACTQ.do(act(W1h[:, :, :, :], W1f.rearrange("p (e c n) -> p e c n", e=NE, c=2), ACT.Copy), c_wa)

            def low_parts():
                POOL.wait(w, gh)
                gl = POOL.do(tt(gWp[:, :, E:2 * E], gWf[:, :].rearrange("p (c e) -> p c e", c=2), gWp[:, :, 0:E],
                                ALU.subtract), c_wp)
                DVE.wait(w1, wa)
                w1l = DVE.do(tt(W1l[:, :, :, :], W1f.rearrange("p (e c n) -> p e c n", e=NE, c=2), W1h[:, :, :, :],
                                ALU.subtract), c_wd)
                return gl, w1l

            def second_weights():
                ACTQ.wait(w2)
                ACTQ.do(act(W2h[:, :], W2f, ACT.Copy), c_wa)
                hi = ACTQ.do(act(b2s[:, :], b2f[:, :], ACT.Copy), c_wa)
                POOL.wait(hi, w2)
                POOL.wait(POOL.do(tt(W2l[:, :], W2f, W2h[:, :], ALU.subtract), c_wp))
                lo = POOL.do(tt(b2s[32:GK, :], b2f[32:GK, :], b2s[32:GK, :], ALU.subtract), c_wp)
                POOL.wait(lo)
                return lo

            up_last, tr_last, gc, gt_read, logit_read, lg_of = {}, {}, {}, {}, {}, {}
            xsplit = {}

            def prep(b):
                y = yield from norm_steps(DVE, c_dve, POOL, c_rs, ST, MV, RS, HALF, XB[b % NX], XN, ld[b], tr_last.get(b - 1))
                if b == 0:
                    yield "normalised"
                for _ in range(Y1):
                    yield
                for t in range(2):
                    for c in range(2):
                        k, bank, free = hring.take()
                        PE.wait(free, y, w)
                        for i in range(4):
                            t_ = PE.do(tr(bank[:, i * 128:(i + 1) * 128], XN[:, 4 * t + i, c * 128:(c + 1) * 128],
                                          ident[:, :]), c_tr if i == 3 else None)
                        sl = slice(t * 512, (t + 1) * 512)
                        ACTQ.wait(t_, up_last.get(b - 2))
                        xh = ACTQ.do(act(XH[b % 2][:, c, sl], bank[:, :], ACT.Copy), c_xh)
                        DVE.wait(xh, up_last.get(b - 2))
                        xl = DVE.do(tt(XL[b % 2][:, c, sl], bank[:, :], XH[b % 2][:, c, sl], ALU.subtract), c_xl)
                        hring.give(k, xl)
                        tr_last[b] = t_
                        yield
                xsplit[b] = xl
                yield
                for t in range(2):
                    sl = slice(t * 512, (t + 1) * 512)
                    k, bank, free = ring.take()
                    PE.wait(free, xl, wa, gl)
                    for c in range(2):
                        PE.do(mm(bank[:, :], gWp[:, c, :], XH[b % 2][:, c, sl], c == 0, False))
                        lt = PE.do(mm(bank[:, :], gWp[:, c, :], XL[b % 2][:, c, sl], False, c == 1), c_lt if c == 1 else None)
                    ACTQ.wait(lt, lg_of.get(b - 1))
                    lc = ACTQ.do(act(LT[:, sl], bank[0:2 * E, :], ACT.Copy), c_lc)
                    ring.give(k, lc)
                    yield
                for _ in range(Y2):
                    yield
                k, bank, free = ring.take()
                PE.wait(free, lc, w)
                for i in range(T):
                    lg_of[b] = PE.do(mm(bank[:, i * E:(i + 1) * E], LT[:, i * 128:(i + 1) * 128],
                                        sel[:, :], True, True), c_lg)
                ACTQ.wait(lg_of[b], logit_read.get(b - 1))
                eg = ACTQ.do(act(EG[:, :], bank[:, 0:T * E], ACT.Exp, scale=-1.0), c_eg)
                ring.give(k, eg)
                yield
                DVE.wait(eg, gt_read.get(b - 1), w)

                def step(f):
                    DVE.wait(DVE.do(f, c_gate))

                def wide(x):
                    return x[:, :].unsqueeze(2).broadcast_to([128, T, E])

                order = desc[:, :].unsqueeze(1).broadcast_to([128, T, E])
                step(ts(EG[:, :], EG[:, :], 1.0, None, ALU.add))
                logit_read[b] = DVE.do(lambda e: e.reciprocal(SC[:, :, :], EG[:, :].rearrange("p (t e) -> p t e", e=E)), c_gate)
                DVE.wait(logit_read[b])
                step(ts(SC[:, :, :], SC[:, :, :], rsc[:, 0:1], None, ALU.mult))
                yield

                def pick(scores, best, hot):
                    step(red(best[:, :], scores[:, :, :], ALU.max))
                    step(tt(EQ[:, :, :], scores[:, :, :], wide(best), ALU.is_equal))
                    yield
                    step(tt(EQ[:, :, :], EQ[:, :, :], order, ALU.mult))
                    step(red(F1[:, :], EQ[:, :, :], ALU.max))
                    step(tt(hot[:, :, :], EQ[:, :, :], wide(F1), ALU.is_equal))

                yield from pick(SC, M1, O1)
                yield
                step(stt(S2[:, :, :], O1[:, :, :], -BIG, SC[:, :, :], ALU.mult, ALU.add))
                yield from pick(S2, M2, O2)
                yield
                step(tt(DN[:, :], M1[:, :], M2[:, :], ALU.add))
                step(lambda e: e.reciprocal(DN[:, :], DN[:, :]))
                step(tt(WA[:, :], M1[:, :], DN[:, :], ALU.mult))
                step(tt(WB[:, :], M2[:, :], DN[:, :], ALU.mult))
                yield
                step(tt(O1[:, :, :], O1[:, :, :], wide(WA), ALU.mult))
                step(tt(O2[:, :, :], O2[:, :, :], wide(WB), ALU.mult))
                step(tt(GF[:, :, :], O1[:, :, :], O2[:, :, :], ALU.add))
                yield
                DVE.wait(ones)
                step(cp(G2[:, :, 0:E], GF[:, :, :]))
                DVE.do(cp(G2[:, :, 32:32 + E], GF[:, :, :]), c_gate)
                DVE.do(cp(G2[:, :, GF0:].bitcast(fp32), GF[:, :, :]), c_gate)
                DVE.do(tt(G2[:, :, E:2 * E], GF[:, :, :], G2[:, :, 0:E], ALU.subtract), c_gate)
                g = DVE.do(tt(G2[:, :, 32 + E:32 + 2 * E], GF[:, :, :], G2[:, :, 0:E], ALU.subtract), c_gate)
                if b == 0:
                    yield "gated"
                for _ in range(Y3):
                    yield
                for t in range(2):
                    k, bank, free = ring.take()
                    PE.wait(free, g)
                    for i in range(4):
                        gt = PE.do(tr(bank[0:GF0 + E, i * 128:(i + 1) * 128], G2[:, 4 * t + i, :].bitcast(fp32), ident[:, :]),
                                   c_gt if i == 3 else None)
                    sl = slice(t * 512, (t + 1) * 512)
                    ACTQ.wait(gt, dn_last.get(b - 2), *(gb_of.get((b - 2, t, e)) for e in range(E)))
                    gr = ACTQ.do(act(GR[b % 2][GF0:, sl], bank[GF0:GF0 + E, :], ACT.Copy), c_gc)
                    gc[b] = ACTQ.do(act(GT[b % 2][:, sl], bank[0:GK, :], ACT.Copy), c_gc)
                    ring.give(k, gc[b])
                    if b == 0:
                        SP.wait(wp2 if t else w1l)
                    for e in range(E):
                        SP.wait(gr, gate_last.get((b - 1, t, e)))
                        gb_of[b, t, e] = SP.do(dma(GB[t][:, e, :], GR[b % 2][GF0 + e:GF0 + e + 1, sl].unsqueeze(1).broadcast_to([1, 128, 512])),
                                            c_gb[t][e], 16)
                gt_read[b] = gt
                yield

            dn_last, dn_of, xo, gb_of, gate_last = {}, {}, {}, {}, {}
            hb_of, gf_of, gl_of = {}, {}, {}
            steps = [(b, t, e) for b in range(NB) for t in range(2) for e in range(NE)]

            def up(n):
                b, t, e = steps[n]
                sl = slice(t * 512, (t + 1) * 512)
                k, bank, free = hring.take()
                PE.wait(free, xsplit[b], wa, w1l)
                for c in range(2):
                    PE.do(mm(bank[:, :], W1l[:, e, c, :], XH[b % 2][:, c, sl], c == 0, False))
                    PE.do(mm(bank[:, :], W1h[:, e, c, :], XL[b % 2][:, c, sl], False, False))
                    u = PE.do(mm(bank[:, :], W1h[:, e, c, :], XH[b % 2][:, c, sl], False, c == 1), c_up if c == 1 else None)
                up_last[b] = u
                if e < E:
                    ACTQ.wait(u, gf_of.get(n - NH))
                    hb_of[n] = ACTQ.do(act(HB[n % NH][:, :], bank[:, :], ACT.Gelu, bias=b1[:, e:e + 1]), c_hb)
                    hring.give(k, hb_of[n])
                else:
                    ACTQ.wait(u, gl_of.get(n - NH))
                    gf_of[n] = ACTQ.do(act(GF32[n % NH][:, :], bank[:, :], ACT.Gelu, bias=b1[:, e:e + 1]), c_hb)
                    hring.give(k, gf_of[n])

            def gate(n):
                b, t, e = steps[n]
                if e < E:
                    DVE.wait(hb_of[n], gb_of[b, t, e], gl_of.get(n - NH))
                    gf_of[n] = DVE.do(tt(GF32[n % NH][:, :], HB[n % NH][:, :], GB[t][:, e, :], ALU.mult), c_gf)
                    gate_last[b, t, e] = gf_of[n]

            def split(n):
                f32, hi, lo = GF32[n % NH], GH[n % NH], GL[n % NH]
                ACTQ.wait(gf_of[n], dn_of.get(n - NH))
                gh = ACTQ.do(act(hi[:, :], f32[:, :], ACT.Copy), c_gh)
                POOL.wait(gh, dn_of.get(n - NH))
                gl_of[n] = POOL.do(tt(lo[:, :], f32[:, :], hi[:, :], ALU.subtract), c_gl)

            def down(n):
                b, t, e = steps[n]
                cols = slice(e * D, (e + 1) * D)
                PE.wait(gl_of[n], wp2)
                for i in range(4):
                    o, tok = PO[:, i * D:(i + 1) * D], slice(i * 128, (i + 1) * 128)
                    if e == 0 and i % 2 == 0:
                        PE.wait(xo.get((n - 1, i // 2)))
                    PE.do(mm(o, GH[n % NH][:, tok], W2h[:, cols], e == 0 and i % 2 == 0, False, True))
                    PE.do(mm(o, GH[n % NH][:, tok], W2l[:, cols], False, False, True))
                    dn_of[n] = PE.do(mm(o, GL[n % NH][:, tok], W2h[:, cols], False, False, True), c_dn)
                if e < NE - 1:
                    return
                for i in range(4):
                    tok = slice(t * 512 + i * 128, t * 512 + (i + 1) * 128)
                    PE.wait(gc[b])
                    dn_last[b] = PE.do(mm(PO[:, i * D:(i + 1) * D], GT[b % 2][:, tok], b2s[:, :], False, True, True), c_dn)
                    if i % 2:
                        x = XB[b % NX][:, 4 * t + i - 1:4 * t + i + 1, :]
                        o = PO[:, (i - 1) * D:(i + 1) * D].rearrange("p (i d) -> p i d", d=D)
                        DVE.wait(dn_last[b])
                        xo[n, i // 2] = DVE.do(stt(x, o, 0.5, x, ALU.mult, ALU.add), c_x)
                if t == 1:
                    SP.wait(xo[n, 1])
                    st[b] = SP.do(dma(rows(dst, b), XB[b % NX][:, :, :]), c_st[b % NX], 16)
                    if b + NX < NB:
                        load(b + NX)

            it = prep(0)
            while next(it) != "normalised":
                pass
            gl, w1l = low_parts()
            while next(it) != "gated":
                pass
            wp2 = second_weights()
            for n in range(AHEAD):
                up(n)
            N = len(steps)
            for n in range(N + LAG):
                if n < N:
                    b, t, e = steps[n]
                    if t == 0 and e == 0:
                        for _ in it:
                            pass
                        it = prep(b + 1) if b + 1 < NB else iter(())
                    if n >= AHEAD:
                        up(n)
                    gate(n)
                next(it, None)
                if 0 < n <= N:
                    split(n - 1)
                if n >= LAG:
                    down(n - LAG)
                next(it, None)
            SP.wait(*(st[b] for b in range(NB - NX, NB)))
            run(PE, ACTQ, DVE, POOL, SP)

    def run(PE, ACTQ, DVE, POOL, SP):
        with nc.Block() as block:
            @block.tensor
            def _(eng):
                PE.play(eng)

            @block.scalar
            def _(eng):
                ACTQ.play(eng)

            @block.vector
            def _(eng):
                DVE.play(eng)

            @block.gpsimd
            def _(eng):
                POOL.play(eng)

            @block.sync
            def _(eng):
                SP.play(eng)

    def attention(src, dst):
        with ExitStack() as local:
            def sb(name, shape, dt):
                return local.enter_context(nc.sbuf_tensor("at" + name, shape, dt))

            def cnt(name):
                return Count(ctx.enter_context(nc.semaphore("at" + name)))

            PE, ACTQ, DVE, POOL, SP = Queue(), Queue(), Queue(), Queue(), Queue()
            WD = [sb("WDq", [128, 2 * 128], fp32), sb("WDkv", [128, 2 * 128], fp32)]
            WU = [sb("WQ", [128, S], fp32), sb("WK", [128, S], fp32)]
            WV, WO = sb("WV", [128, S], fp32), sb("WO", [128, NP * D], fp32)
            COS, SIN = sb("COS", [128, S], fp32), sb("SIN", [128, S], fp32)
            lns = sb("lns", [128, 4], fp32)
            ident, identb, ones = sb("ident", [128, 128], fp32), sb("identb", [128, 128], bf16), sb("ones", [128, 64], fp32)
            XB = [sb(f"XB{i}", [128, T, D], fp32) for i in range(2)]
            Y = sb("Y", [128, T, D], fp32)
            ST, MV, RS = sb("ST", [128, T, 6], fp32), sb("MV", [128, T, 2], fp32), sb("RS", [128, T], fp32)
            HALF = sb("HALF", [128, T], fp32)
            C = [sb("CQ", [128, S], fp32), sb("CKV", [128, S], fp32)]
            U = sb("U", [128, 2, S], fp32)
            R = [sb(f"R{i}", [128, 512], fp32) for i in range(2)]
            VT = [sb(f"VT{i}", [128, 512], fp32) for i in range(2)]
            QA = [[sb(f"QA{i}{h}", [128, S], fp32r) for h in range(2)] for i in range(2)]
            QB = [[sb(f"QB{i}{h}", [128, S], fp32r) for h in range(2)] for i in range(2)]
            KA = [[sb(f"KA{i}{h}", [128, S], fp32r) for h in range(2)] for i in range(2)]
            KB = [[sb(f"KB{i}{h}", [128, S], fp32r) for h in range(2)] for i in range(2)]
            V = [sb(f"V{i}", [128, T, 128], fp32) for i in range(2)]
            PT = [[sb(f"PT{i}{h}", [128, S], fp32) for h in range(2)] for i in range(3)]
            ACC = [[sb(f"ACC{i}{h}", [128, S], fp32) for h in range(2)] for i in range(2)]
            RSUM = sb("RSUM", [128, S], fp32)
            AT = sb("AT", [128, GP, S], fp32)
            NM, MF = sb("NM", [128, 16, 2], fp32), sb("MF", [128, 16], fp32)
            MC = sb("MC", [128, 16, 2], bf16)

            c_w, c_ld, c_st = [cnt(f"w{i}") for i in range(3)], [cnt("ld0"), cnt("ld1")], [cnt("st0"), cnt("st1")]
            c_ini, c_dve, c_rs, c_res, c_res0 = cnt("ini"), cnt("dve"), cnt("rs"), cnt("res"), cnt("res0")
            c_tr, c_ht, c_dp, c_c = cnt("tr"), cnt("ht"), cnt("dp"), cnt("c")
            c_up, c_raw, c_sw, c_rope, c_rot, c_hi, c_lo, c_lp = cnt("up"), cnt("raw"), [cnt("sw0"), cnt("sw1")], cnt("rope"), cnt("rot"), cnt("hi"), cnt("lo"), cnt("lp")
            c_vp, c_v, c_mx, c_nm, c_mr, c_mrow = cnt("vp"), cnt("v"), cnt("mx"), cnt("nm"), cnt("mr"), cnt("mrow")
            c_qk, c_exp, c_pv, c_acc, c_o = cnt("qk"), cnt("exp"), cnt("pv"), cnt("acc"), cnt("o")
            c_sum, c_rs2, c_rec, c_at, c_op, c_x = cnt("sum"), cnt("rs2"), cnt("rec"), cnt("atn"), cnt("op"), cnt("x")

            ring = Ring(PM)
            ld, st = {}, {}

            def load(b):
                SP.wait(st.get(b - 2))
                ld[b] = SP.do(dma(XB[b % 2][:, :, :], rows(src, b)), c_ld[b % 2], 16)

            load(0)

            def weights(count, *tensors):
                for t, name in tensors:
                    mark = SP.do(dma(t[:, :], a[name]), count, 16)
                return mark

            w = weights(c_w[0], (ident, "ident"), (lns, "ln"), (WD[0], "wdq"), (WD[1], "wdkv"))
            wu = weights(c_w[1], (WU[0], "wq"), (WU[1], "wk"), (COS, "cos"), (SIN, "sin"))
            wv = weights(c_w[2], (WV, "wv"), (WO, "wo"))
            load(1)
            POOL.wait(POOL.do(lambda e: e.memset(HALF[:, :], -0.5), c_ini))

            def constants():
                POOL.wait(POOL.last)
                for i in range(2):
                    POOL.do(lambda e, i=i: e.memset(KB[i][0][64:96, :].bitcast(fp32), 1.0), c_ini)
                    POOL.do(lambda e, i=i: e.memset(QB[i][1][0:64, :].bitcast(fp32), 0.0), c_ini)
                    z = POOL.do(lambda e, i=i: e.memset(KB[i][1][0:64, :].bitcast(fp32), 0.0), c_ini)
                    POOL.wait(z)
                    POOL.do(lambda e, i=i: e.memset(KB[i][1][0:2, :].bitcast(fp32), 1.0), c_ini)
                POOL.do(lambda e: e.memset(ones[:, :], 1.0), c_ini)
                POOL.wait(w)
                return POOL.do(cp(identb[:, :], ident[:, :]), c_ini)

            HI = [slice(0, 64), slice(64, 128)]
            KR = [slice(0, 66), slice(0, 128)]
            MROW = [slice(64, 66), slice(0, 2)]
            y_of, res_of, c_of, up_of, lo_of, hi_of, dp_of = {}, {}, {}, {}, {}, {}, {}
            ready, v_of, qk_of, pv_of, mr_of, sum_of, op_of, at_of, o_of, nm_of = {}, {}, {}, {}, {}, {}, {}, {}, {}, {}
            last_rope, last_swap, rot_of, tr_of = [None, None], [None, None], {}, {}

            def lows(n):
                return [lo_of.get((n, i)) for i in range(4)]

            def norms(b):
                y = yield from norm_steps(DVE, c_dve, POOL, c_rs, ST, MV, RS, HALF, XB[b % 2], Y, ld[b], tr_of.get(b - 1))

                def residual():
                    eng, count = (POOL, c_res) if b else (DVE, c_res0)
                    eng.wait(y)
                    res_of[b] = eng.do(tt(XB[b % 2][:, :, :], XB[b % 2][:, :, :], Y[:, :, :], ALU.add), count)
                    return res_of[b]

                DVE.wait(y)
                y_of[b] = yield from norm_steps(DVE, c_dve, POOL, c_rs, ST, MV, RS, HALF, Y, Y, None, None, residual)

            def latents(b):
                n0 = 8 * b - 1
                for t in range(2):
                    sl = slice(t * 512, (t + 1) * 512)
                    for c in range(2):
                        k, bank, free = ring.take()
                        PE.wait(free, y_of[b], w)
                        for i in range(4):
                            tr_of[b] = PE.do(tr(bank[:, i * 128:(i + 1) * 128], Y[:, 4 * t + i, c * 128:(c + 1) * 128],
                                                ident[:, :]), c_tr if i == 3 else None)
                        ACTQ.wait(tr_of[b], w, *lows(n0), hi_of.get(n0))
                        ht = ACTQ.do(act(U[:, c, sl], bank[:, :], ACT.Identity, scale=lns[:, c:c + 1],
                                         bias=lns[:, 2 + c:3 + c]), c_ht)
                        ring.give(k, ht)
                        yield
                for t in range(2):
                    sl = slice(t * 512, (t + 1) * 512)
                    for m in range(2):
                        k, bank, free = ring.take()
                        PE.wait(free, ht)
                        for c in range(2):
                            dp_of[b] = PE.do(mm(bank[:, :], WD[m][:, c * 128:(c + 1) * 128], U[:, c, sl], c == 0, c == 1),
                                             c_dp if c == 1 else None)
                        ACTQ.wait(dp_of[b], up_of.get(n0))
                        c_of[b] = ACTQ.do(act(C[m][:, sl], bank[:, :], ACT.Copy), c_c)
                        ring.give(k, c_of[b])
                        yield

            def rotate(n):
                b, p = divmod(n, NP)
                cols = slice(p * 128, (p + 1) * 128)

                def first(m, t):
                    sl = slice(t * 512, (t + 1) * 512)
                    k, bank, free = ring.take()
                    PE.wait(free, c_of[b], wu)
                    up_of[n] = PE.do(mm(bank[:, :], WU[m][:, cols], C[m][:, sl], True, True), c_up)
                    ACTQ.wait(up_of[n], last_swap[t])
                    raw = ACTQ.do(act(R[t][:, :], bank[:, :], ACT.Copy), c_raw)
                    SP.wait(raw, last_rope[t])
                    for i in range(2):
                        last_swap[t] = SP.do(dma(VT[t][1 - i:128:2, :], R[t][i:128:2, :]), c_sw[t], 16)
                    DVE.wait(raw, wu, dp_of[b], *lows(n - 1), hi_of.get(n - 1))
                    ring.give(k, DVE.do(tt(U[:, m, sl], bank[:, :], COS[:, sl], ALU.mult), c_rope))

                def second(m, t):
                    sl = slice(t * 512, (t + 1) * 512)
                    DVE.wait(last_swap[t], wu)
                    rope = DVE.do(tt(VT[t][:, :], VT[t][:, :], SIN[:, sl], ALU.mult), c_rope)
                    DVE.wait(rope)
                    last_rope[t] = rot_of[n, m] = DVE.do(tt(U[:, m, sl], U[:, m, sl], VT[t][:, :], ALU.add), c_rot)

                for step, m, t in ((first, 0, 0), (first, 0, 1), (second, 0, 0), (first, 1, 0), (second, 0, 1),
                                   (first, 1, 1), (second, 1, 0), (second, 1, 1)):
                    step(m, t)
                    yield

            def highs(n):
                s = n % 2
                for m, A in ((0, QA), (1, KA)):
                    for h in range(2):
                        ACTQ.wait(rot_of[n, m], qk_of.get(n - 2))
                        hi_of[n, m, h] = ACTQ.do(act(A[s][h][HI[h], :], U[HI[h], m, :], ACT.Copy), c_hi)
                        yield

            def parts(n):
                s = n % 2
                ACTQ.wait(ini)
                for h in range(2):
                    ACTQ.do(act(QA[s][h][HI[1 - h], :], U[HI[h], 0, :], ACT.Copy), c_hi)
                    yield
                    DVE.wait(hi_of[n, 0, h], qk_of.get(n - 2), ini)
                    lo_of[n, 2 + h] = DVE.do(tt(QB[s][h][HI[h], :], U[HI[h], 0, :], QA[s][h][HI[h], :], ALU.subtract), c_lo)
                    yield
                    hi_of[n] = ACTQ.do(act(KB[s][h][HI[h], :], U[HI[h], 1, :], ACT.Copy), c_hi)
                    yield
                    POOL.wait(hi_of[n, 1, h], qk_of.get(n - 2), ini, POOL.last)
                    lo_of[n, h] = POOL.do(tt(KA[s][h][HI[1 - h], :], U[HI[h], 1, :], KA[s][h][HI[h], :], ALU.subtract), c_lp)
                    POOL.wait(lo_of[n, h])
                    yield

            def values(n):
                b, p = divmod(n, NP)
                cols = slice(p * 128, (p + 1) * 128)
                for t in range(2):
                    k, bank, free = ring.take()
                    PE.wait(free, c_of[b], wv)
                    for i in range(4):
                        vp = PE.do(mm(bank[:, i * 128:(i + 1) * 128], C[1][:, (4 * t + i) * 128:(4 * t + i + 1) * 128],
                                      WV[:, cols], True, True), c_vp if i == 3 else None)
                    ACTQ.wait(vp, pv_of.get(n - 2))
                    v_of[n] = ACTQ.do(act(V[n % 2][:, 4 * t:4 * t + 4, :], bank[:, :].rearrange("p (i d) -> p i d", d=128),
                                          ACT.Copy), c_v)
                    ring.give(k, v_of[n])
                    up_of[n] = vp
                    yield

            def maxima(n):
                s = n % 2
                PE.wait(hi_of[n, 1, 1])
                for q in range(T):
                    for t in range(2):
                        for h in range(2):
                            k, bank, free = ring.take()
                            PE.wait(free)
                            mx = PE.do(mm(bank[:, :], QA[s][h][HI[h], q * 128:(q + 1) * 128],
                                          KA[s][h][HI[h], t * 512:(t + 1) * 512], True, True), c_mx)
                            DVE.wait(mx, nm_of.get(n - 1))
                            nm = DVE.do(red(NM[:, h * T + q, t:t + 1], bank[:, :], ALU.max, True), c_nm)
                            ring.give(k, nm)
                            yield
                DVE.wait(nm, mr_of.get(n - 1))
                f = DVE.do(red(MF[:, :], NM[:, :, :], ALU.min), c_nm)
                DVE.wait(f)
                f = DVE.do(cp(MC[:, :, 0], MF[:, :]), c_nm)
                DVE.wait(f)
                nm_of[n] = DVE.do(tt(MC[:, :, 1], MF[:, :], MC[:, :, 0], ALU.subtract), c_nm)
                yield
                for t in range(2):
                    k, bank, free = ring.take()
                    PE.wait(free, nm_of[n], ini)
                    for q in range(4):
                        for h in range(2):
                            mr_of[n] = PE.do(mm(bank[MROW[h], q * 128:(q + 1) * 128], MC[:, h * T + 4 * t + q, :],
                                                identb[:, :], True, True), c_mr if q == 3 and h == 1 else None)
                    ACTQ.wait(mr_of[n])
                    for h in range(2):
                        row = ACTQ.do(act(QB[s][h][MROW[h], t * 512:(t + 1) * 512], bank[MROW[h], :], ACT.Copy), c_mrow)
                    ring.give(k, row)
                    yield
                ready[n] = (row, hi_of[n], *lows(n))

            def sums(n):
                for t in range(2):
                    sl = slice(t * 512, (t + 1) * 512)
                    k, bank, free = ring.take()
                    PE.wait(free, acc_of[n], ini)
                    for h in range(2):
                        sum_of[n] = PE.do(mm(bank[HI[h], :], ones[:, :], ACC[n % 2][h][:, sl], True, True),
                                          c_sum if h == 1 else None)
                    ACTQ.wait(sum_of[n], at_of.get((n - 1, t)))
                    rs_of[n, t] = ACTQ.do(act(RSUM[:, sl], bank[:, :], ACT.Copy), c_rs2)
                    ring.give(k, rs_of[n, t])
                    yield

            def divide(n):
                for t in range(2):
                    for u in range(2):
                        sl = slice(t * 512 + u * 256, t * 512 + (u + 1) * 256)
                        DVE.wait(rs_of[n, t])
                        rec = DVE.do(lambda e, sl=sl: e.reciprocal(RSUM[:, sl], RSUM[:, sl]), c_rec)
                        yield
                    sl = slice(t * 512, (t + 1) * 512)
                    DVE.wait(rec, o_of[n, t])
                    o = AT[:, n % GP, sl]
                    at_of[n, t] = DVE.do(tt(o, o, RSUM[:, sl], ALU.mult), c_at)
                    yield

            def outward(n):
                b, p = divmod(n, NP)
                for u in range(4):
                    k, bank, free = ring.take()
                    PE.wait(free, at_of[n, u // 2], wv)
                    for i in range(2):
                        for q in range(GP):
                            tok = slice((2 * u + i) * 128, (2 * u + i + 1) * 128)
                            op_of[n] = PE.do(mm(bank[:, i * D:(i + 1) * D], AT[:, q, tok],
                                                WO[:, (p - GP + 1 + q) * D:(p - GP + 2 + q) * D], q == 0, q == GP - 1),
                                             c_op if i == 1 and q == GP - 1 else None)
                    x = XB[b % 2][:, 2 * u:2 * u + 2, :]
                    DVE.wait(op_of[n], res_of[b], x_of.get((b, u)))
                    x_of[b, u] = DVE.do(tt(x, x, bank[:, :].rearrange("p (i d) -> p i d", d=D), ALU.add), c_x)
                    ring.give(k, x_of[b, u])
                    yield
                if p == NP - 1:
                    SP.wait(x_of[b, 3])
                    st[b] = SP.do(dma(rows(dst, b), XB[b % 2][:, :, :]), c_st[b % 2], 16)
                    if b + 2 < NB:
                        load(b + 2)

            acc_of, x_of, rs_of = {}, {}, {}
            sring = Ring(PS)
            pt_pv, pt_acc = {}, {}

            NN = NB * NP
            plan = []

            def due(m, work, steps, first, last):
                plan.append([work, steps, 32 * (m - 1) + first, 32 * (m - 1) + last, 0])

            for m in range(NN):
                b, p = divmod(m, NP)
                d = DD if p == 0 else 0
                if p == 0 and b:
                    due(m, norms(b), 22, *P["norms"])
                if p == 0:
                    due(m, latents(b), 8, *P["latents"])
                for name, work, steps in (("rotate", rotate, 8), ("highs", highs, 4), ("parts", parts, 8),
                                          ("values", values, 2), ("maxima", maxima, 35)):
                    x, y = P[name]
                    due(m, work(m), steps, min(x + d, y if name == "maxima" else 99), y + (0 if name == "maxima" else d))
                due(m, sums(m), 2, *P["sums"])
                due(m, divide(m), 6, *P["divide"])
                if p % GP == GP - 1:
                    due(m, outward(m), 4, *P["outward"])

            def fill(k):
                for x in plan:
                    work, steps, first, last, done = x
                    if k >= first:
                        n = steps if k >= last else steps * (k - first + 1) // (last - first + 1)
                        for _ in range(n - done):
                            next(work, None)
                        x[4] = max(n, done)
                        if k >= last:
                            for _ in work:
                                pass
                plan[:] = [x for x in plan if k < x[3]]

            exps = {}

            def pv(base, t):
                n, j = divmod(base, T)
                p, sl = n % NP, slice(t * 512, (t + 1) * 512)
                PE.wait(v_of[n], o_of.get((n - 1, t)), exps[base, 0, t], exps[base, 1, t])
                for h in range(2):
                    pv_of[n] = PE.do(mm(PO[HI[h], sl], V[n % 2][:, j, HI[h]], PT[base % 3][h][:, sl], j == 0, j == T - 1),
                                     c_pv if h == 1 else None)
                if t == 1:
                    pt_pv[base] = pv_of[n]
                if j == T - 1:
                    ACTQ.wait(pv_of[n], op_of.get(n - 1 - p % GP))
                    o_of[n, t] = ACTQ.do(act(AT[:, p % GP, sl], PO[:, sl], ACT.Copy), c_o)

            for _ in norms(0):
                pass
            ini = constants()
            for k in range(-64, 0):
                fill(k)
            for n in range(NN):
                b, p = divmod(n, NP)
                s = n % 2
                for j in range(T):
                    base = n * T + j
                    for h in range(2):
                        for t in range(2):
                            sl = slice(t * 512, (t + 1) * 512)
                            k, bank, free = sring.take()
                            PE.wait(free, *ready[n])
                            PE.do(mm(bank[:, :], KA[s][h][:, j * 128:(j + 1) * 128], QA[s][h][:, sl], True, False))
                            qk_of[n] = PE.do(mm(bank[:, :], KB[s][h][KR[h], j * 128:(j + 1) * 128], QB[s][h][KR[h], sl],
                                                False, True), c_qk)
                            ACTQ.wait(qk_of[n], pt_pv.get(base - 3), pt_acc.get(base - 3))
                            exps[base, h, t] = ACTQ.do(act(PT[base % 3][h][:, sl], bank[:, :], ACT.Exp, scale=SCALE), c_exp)
                            sring.give(k, exps[base, h, t])
                        fill(32 * n + 4 * j + 2 * h)
                        if base:
                            pv(base - 1, h)
                        fill(32 * n + 4 * j + 2 * h + 1)
                    if j >= 1:
                        for h in range(2):
                            POOL.wait(exps[base, h, 1], sum_of.get(n - 2), pt_acc.get(base - 1) if j > 1 else None)
                            first = PT[(base - 1) % 3][h] if j == 1 else ACC[s][h]
                            pt_acc[base] = POOL.do(tt(ACC[s][h][:, :], first[:, :], PT[base % 3][h][:, :], ALU.add), c_acc)
                        if j == 1:
                            pt_acc[base - 1] = pt_acc[base]
                        acc_of[n] = pt_acc[base]
            for t in range(2):
                pv(NN * T - 1, t)
            for k in range(32 * NN, 32 * NN + 64):
                fill(k)
            SP.wait(st[NB - 2], st[NB - 1])
            run(PE, ACTQ, DVE, POOL, SP)

    ffn("f1", a["x"], x1)
    attention(x1, x2)
    ffn("f2", x2, out)


def _tables(np):
    inv = 1.0 / 10000.0 ** (np.arange(0, 64, 2, dtype=np.float32) / 64)
    freqs = np.outer(np.arange(1024, dtype=np.float32), inv)
    cos = np.concatenate([np.cos(freqs), np.cos(freqs)], -1)[:, ::2]
    sin = np.concatenate([np.sin(freqs), np.sin(freqs)], -1)[:, ::2]
    dim = np.arange(128) % 64 // 2
    sign = np.where(np.arange(128) % 2 == 0, -1.0, 1.0).astype(np.float32)
    return cos[:, dim].T.astype(np.float32), (sin[:, dim].T * sign[:, None]).astype(np.float32)


def kernel(**inputs):
    import numpy as np
    import concourse.bacc as _bacc
    from concourse import mybir as _mybir
    from concourse.bass_utils import run_bass_kernel_spmd as _run

    v = {k: np.asarray(x) for k, x in inputs.items()}
    f = {k[7:]: x for k, x in v.items() if k.startswith("L0_ffn_")}
    t = {k[8:]: x for k, x in v.items() if k.startswith("L0_attn_")}
    cos, sin = _tables(np)
    sel = np.concatenate([np.eye(8), np.eye(8)]).astype(np.float32)

    def chunks(w):
        return w.reshape(-1, 128, w.shape[1]).transpose(1, 0, 2).reshape(128, -1)

    w1 = np.concatenate([f["W1"], f["Ws1"][None]])
    w2 = np.concatenate([f["W2"], f["Ws2"][None]])
    b2 = np.concatenate([f["b2"], f["b2"], f["bs2"][None]])
    ln = np.concatenate([t["ln_scale"].reshape(2, 128), t["ln_bias"].reshape(2, 128)])
    arrays = {
        "x": t["x"].reshape(8192, 256),
        "W1": w1.reshape(9, 2, 128, 128).transpose(2, 0, 1, 3).reshape(128, -1),
        "W2": w2.transpose(1, 0, 2).reshape(128, -1),
        "gate": chunks(f["gate_W"]),
        "b1": np.concatenate([f["b1"], f["bs1"][None]]).T,
        "b2": np.concatenate([b2, np.zeros((15, 256), np.float32), b2]),
        "rs": np.broadcast_to(f["route_scale"].reshape(1, 1), (128, 1)),
        "desc": np.broadcast_to(np.arange(8, 0, -1, dtype=np.float32), (128, 8)),
        "sel": sel,
        "ident": np.eye(128, dtype=np.float32),
        "ln": ln.T,
        "wdq": chunks(t["w_down_q"].T),
        "wdkv": chunks(t["w_down_kv"].T),
        "wq": t["w_up_q"].T,
        "wk": t["w_up_k"].T,
        "wv": t["w_up_v"].T,
        "wo": chunks(t["w_out"].T),
        "cos": cos,
        "sin": sin,
    }
    nc = _bacc.Bacc("TRN2", target_bir_lowering=False, num_devices=1)
    args, maps = {}, {}
    for name, x in arrays.items():
        x = np.ascontiguousarray(x)
        maps["in_" + name] = x
        args[name] = nc.dram_tensor("in_" + name, x.shape, _mybir.dt.from_np(x.dtype), kind="ExternalInput").ap()
    out = nc.dram_tensor("out_0", (8192, 256), _mybir.dt.float32, kind="ExternalOutput").ap()
    macaron_kernel(nc, args, out)
    r = _run(nc, [maps], core_ids=[0])
    return r.results[0]["out_0"].reshape(8, 1024, 256)
```
